# Optimizing a Trainium2 kernel written in Bass

```python
import numpy as np
import jax
import jax.numpy as jnp

def _softmax(x, axis=-1):
    return jax.nn.softmax(x, axis=axis)
def _gelu(x):
    return jax.nn.gelu(x, approximate=True)
def _silu(x):
    return jax.nn.silu(x)
def _sigmoid(x):
    return jax.nn.sigmoid(x)
def _layernorm(x, axis=-1, eps=1e-5):
    m = jnp.mean(x, axis=axis, keepdims=True)
    v = jnp.var(x, axis=axis, keepdims=True)
    return (x - m) / jnp.sqrt(v + eps)
def _scatter_add(tgt, idx, src, axis=0):
    return tgt.at[idx].add(src)
def _segment_sum(src, seg, n):
    return jax.ops.segment_sum(src, seg, n)

kernel_name = 'mk_conv_preact_d4_conv_nhwc128_7f87bb'

def setup_inputs(seed: int = 0):
    np.random.seed(seed)
    _w = jnp.asarray
    def _rec_inputs():
        import jax
        import jax.numpy as jnp
        _gk = jax.random.key(seed)
        x = 7.22e-05 + 1 * jax.random.normal(jax.random.fold_in(_gk, 1), (1, 256, 256, 128), jnp.float32)
        return x
    x = _rec_inputs()
    def _L0_conv_setup():
        import math
        import jax, jax.numpy as jnp
        import numpy as np
        H = 4
        C_HID = 32
        key = jax.random.key(seed)
        ks = jax.random.split(key, 8)
        B, N, C = (1, 256, 128)
        q_x = jax.random.normal(ks[0], (B, N, N, C), dtype=jnp.float32)
        kv_x = jax.random.normal(ks[1], (B, N, N, C), dtype=jnp.float32)
        tri_bias = jax.random.normal(ks[2], (B, 1, H, N, N), dtype=jnp.float32)
        mask_bias = jnp.zeros((B, N, 1, 1, N), dtype=jnp.float32)
        mask = jnp.ones((B, N, N, N), dtype=jnp.float32)
        s = 1.0 / math.sqrt(C)
        Wq = jax.random.normal(ks[3], (C, H * C_HID), dtype=jnp.float32) * s
        Wk = jax.random.normal(ks[4], (C, H * C_HID), dtype=jnp.float32) * s
        Wv = jax.random.normal(ks[5], (C, H * C_HID), dtype=jnp.float32) * s
        Wg = jax.random.normal(ks[6], (C, H * C_HID), dtype=jnp.float32) * s
        Wo = jax.random.normal(ks[7], (H * C_HID, C), dtype=jnp.float32) * s
        return {'q_x': q_x, 'kv_x': kv_x, 'tri_bias': tri_bias, 'mask_bias': mask_bias, 'mask': mask, 'Wq': Wq, 'Wk': Wk, 'Wv': Wv, 'Wg': Wg, 'Wo': Wo}
    _L0_conv_all = _L0_conv_setup()
    _L0_conv_in = {k: v for k, v in _L0_conv_all.items() if k in ('kv_x', 'tri_bias', 'mask_bias', 'mask', 'Wq', 'Wk', 'Wv', 'Wg', 'Wo', )}
    del _L0_conv_all

    def _L1_conv_setup():
        import jax, jax.numpy as jnp
        import numpy as np
        LN_EPS = 1e-05

        def _layer_norm(h, g, b):
            mu = jnp.mean(h, axis=-1, keepdims=True)
            var = jnp.mean(jnp.square(h - mu), axis=-1, keepdims=True)
            return (h - mu) * jax.lax.rsqrt(var + LN_EPS) * g + b

        def _forward_fourier(x, w1, w2):
            xt = jnp.transpose(x, (0, 3, 1, 2))
            B, I, M, N = xt.shape
            nm = w1.shape[2]
            cw1 = w1[..., 0] + 1j * w1[..., 1]
            cw2 = w2[..., 0] + 1j * w2[..., 1]
            O = cw1.shape[1]
            fty = jnp.fft.rfft(xt, axis=-1, norm='ortho')
            f1 = jnp.einsum('bixy,ioy->boxy', fty[..., :nm], cw1)
            pad_y = jnp.zeros((B, O, M, N // 2 + 1 - nm), dtype=f1.dtype)
            xy = jnp.fft.irfft(jnp.concatenate([f1, pad_y], axis=-1), n=N, axis=-1, norm='ortho')
            ftx = jnp.fft.rfft(xt, axis=-2, norm='ortho')
            f2 = jnp.einsum('bixy,iox->boxy', ftx[:, :, :nm, :], cw2)
            pad_x = jnp.zeros((B, O, M // 2 + 1 - nm, N), dtype=f2.dtype)
            xx = jnp.fft.irfft(jnp.concatenate([f2, pad_x], axis=-2), n=M, axis=-2, norm='ortho')
            return jnp.transpose(xx + xy, (0, 2, 3, 1))
        key = jax.random.key(seed)
        ks = jax.random.split(key, 6)
        B, M, N, D = (16, 128, 128, 128)
        NM, H = (16, 512)
        xav = float(np.sqrt(2.0 / (D + D)))
        return {'x': jax.random.normal(ks[0], (B, M, N, D), jnp.float32), 'w1': jax.random.normal(ks[1], (D, D, NM, 2), jnp.float32) * xav, 'w2': jax.random.normal(ks[2], (D, D, NM, 2), jnp.float32) * xav, 'ff_w0': jax.random.normal(ks[3], (D, H), jnp.float32) * float(1.0 / np.sqrt(D)), 'ff_b0': jnp.zeros((H,), jnp.float32), 'ff_w1': jax.random.normal(ks[4], (H, D), jnp.float32) * float(1.0 / np.sqrt(H)), 'ff_b1': jnp.zeros((D,), jnp.float32), 'ln_g': jnp.ones((D,), jnp.float32), 'ln_b': jnp.zeros((D,), jnp.float32)}
    _L1_conv_all = _L1_conv_setup()
    _L1_conv_in = {k: v for k, v in _L1_conv_all.items() if k in ('w1', 'w2', 'ff_w0', 'ff_b0', 'ff_w1', 'ff_b1', 'ln_g', 'ln_b', )}
    del _L1_conv_all

    def _L2_conv_setup():
        import jax, jax.numpy as jnp
        import numpy as np
        from jax import lax
        DN = ('NHWC', 'HWIO', 'NHWC')
        key = jax.random.key(seed)
        k0, k1, k2 = jax.random.split(key, 3)
        B, H, W, C, D = (8, 128, 256, 128, 128)
        x = jax.random.normal(k0, (B, H, W, C), jnp.float32)
        w1 = jax.random.normal(k1, (1, 9, C, 1), jnp.float32) * 0.05
        b1 = jnp.zeros((1,), jnp.float32)
        w2 = jax.random.normal(k2, (1, 9, C, D), jnp.float32) * 0.05
        b2 = jnp.zeros((D,), jnp.float32)
        return {'x': x, 'w1': w1, 'b1': b1, 'w2': w2, 'b2': b2}
    _L2_conv_all = _L2_conv_setup()
    _L2_conv_in = {k: v for k, v in _L2_conv_all.items() if k in ('w1', 'b1', 'w2', 'b2', )}
    del _L2_conv_all

    def _L3_conv_setup():
        import jax, jax.numpy as jnp
        import numpy as np
        EPS = 1e-06

        def kernel_to_freq_2d(kernel, H, W):
            C, kh, kw = kernel.shape
            th = (jnp.arange(kh) - kh // 2) % H
            tw = (jnp.arange(kw) - kw // 2) % W
            TH, TW = jnp.meshgrid(th, tw, indexing='ij')
            padded = jnp.zeros((C, H, W), dtype=kernel.dtype).at[:, TH, TW].set(kernel)
            return jnp.fft.fft2(padded, axes=(1, 2))

        def heinsen_scan_log(log_coeffs, log_values):

            def op(left, right):
                la, lb = left
                ra, rb = right
                return (la + ra, jnp.logaddexp(ra + lb, rb))
            _, log_h = jax.lax.associative_scan(op, (log_coeffs, log_values), axis=0)
            return log_h
        key = jax.random.key(seed)
        ks = jax.random.split(key, 7)
        B, H, W, C, k = (4, 128, 128, 128, 7)
        fan_in = k * k
        x = jax.random.normal(ks[0], (B, H, W, C), dtype=jnp.float32)
        A_kernel = jax.random.normal(ks[1], (C, k, k), dtype=jnp.float32) / np.sqrt(fan_in)
        B_kernel = jax.random.normal(ks[2], (C, k, k), dtype=jnp.float32) / np.sqrt(fan_in)
        gate_A_kernel = jax.random.normal(ks[3], (C, k, k), dtype=jnp.float32) * 0.02
        gate_B_kernel = jax.random.normal(ks[4], (C, k, k), dtype=jnp.float32) * 0.02
        W_out = jax.random.normal(ks[5], (C, C), dtype=jnp.float32) / np.sqrt(C)
        b_out = jnp.zeros((C,), dtype=jnp.float32)
        return dict(x=x, A_kernel=A_kernel, B_kernel=B_kernel, gate_A_kernel=gate_A_kernel, gate_B_kernel=gate_B_kernel, W_out=W_out, b_out=b_out, T=8)
    _L3_conv_all = _L3_conv_setup()
    _L3_conv_in = {k: v for k, v in _L3_conv_all.items() if k in ('A_kernel', 'B_kernel', 'gate_A_kernel', 'gate_B_kernel', 'W_out', 'b_out', )}
    del _L3_conv_all

    return {
        "x": x,
        "L0_conv_kv_x": _L0_conv_in["kv_x"],
        "L0_conv_tri_bias": _L0_conv_in["tri_bias"],
        "L0_conv_mask_bias": _L0_conv_in["mask_bias"],
        "L0_conv_mask": _L0_conv_in["mask"],
        "L0_conv_Wq": _L0_conv_in["Wq"],
        "L0_conv_Wk": _L0_conv_in["Wk"],
        "L0_conv_Wv": _L0_conv_in["Wv"],
        "L0_conv_Wg": _L0_conv_in["Wg"],
        "L0_conv_Wo": _L0_conv_in["Wo"],
        "L1_conv_w1": _L1_conv_in["w1"],
        "L1_conv_w2": _L1_conv_in["w2"],
        "L1_conv_ff_w0": _L1_conv_in["ff_w0"],
        "L1_conv_ff_b0": _L1_conv_in["ff_b0"],
        "L1_conv_ff_w1": _L1_conv_in["ff_w1"],
        "L1_conv_ff_b1": _L1_conv_in["ff_b1"],
        "L1_conv_ln_g": _L1_conv_in["ln_g"],
        "L1_conv_ln_b": _L1_conv_in["ln_b"],
        "L2_conv_w1": _L2_conv_in["w1"],
        "L2_conv_b1": _L2_conv_in["b1"],
        "L2_conv_w2": _L2_conv_in["w2"],
        "L2_conv_b2": _L2_conv_in["b2"],
        "L3_conv_A_kernel": _L3_conv_in["A_kernel"],
        "L3_conv_B_kernel": _L3_conv_in["B_kernel"],
        "L3_conv_gate_A_kernel": _L3_conv_in["gate_A_kernel"],
        "L3_conv_gate_B_kernel": _L3_conv_in["gate_B_kernel"],
        "L3_conv_W_out": _L3_conv_in["W_out"],
        "L3_conv_b_out": _L3_conv_in["b_out"],
    }

def reference(x, L0_conv_kv_x, L0_conv_tri_bias, L0_conv_mask_bias, L0_conv_mask, L0_conv_Wq, L0_conv_Wk, L0_conv_Wv, L0_conv_Wg, L0_conv_Wo, L1_conv_w1, L1_conv_w2, L1_conv_ff_w0, L1_conv_ff_b0, L1_conv_ff_w1, L1_conv_ff_b1, L1_conv_ln_g, L1_conv_ln_b, L2_conv_w1, L2_conv_b1, L2_conv_w2, L2_conv_b2, L3_conv_A_kernel, L3_conv_B_kernel, L3_conv_gate_A_kernel, L3_conv_gate_B_kernel, L3_conv_W_out, L3_conv_b_out):
    import jax
    import jax.numpy as jnp
    def _L0_conv_ref(q_x, kv_x, tri_bias, mask_bias, mask, Wq, Wk, Wv, Wg, Wo):
        import math
        import jax, jax.numpy as jnp
        import numpy as np
        H = 4
        C_HID = 32
        lead = q_x.shape[:-1]

        def split_heads(t):
            t = t.reshape(t.shape[:-1] + (H, C_HID))
            return jnp.swapaxes(t, -2, -3)
        q = split_heads(q_x @ Wq) / math.sqrt(C_HID)
        k = split_heads(kv_x @ Wk)
        v = split_heads(kv_x @ Wv)
        a = jnp.einsum('bnhqc,bnhkc->bnhqk', q, k)
        a = a + mask_bias + tri_bias
        a = jax.nn.softmax(a, axis=-1)
        o = jnp.einsum('bnhqk,bnhkc->bnhqc', a, v)
        o = jnp.swapaxes(o, -2, -3)
        g = jax.nn.sigmoid(q_x @ Wg).reshape(lead + (H, C_HID))
        o = o * g
        o = o.reshape(lead + (H * C_HID,))
        return o @ Wo

    def _L1_conv_ref(x, w1, w2, ff_w0, ff_b0, ff_w1, ff_b1, ln_g, ln_b):
        import jax, jax.numpy as jnp
        import numpy as np
        LN_EPS = 1e-05

        def _layer_norm(h, g, b):
            mu = jnp.mean(h, axis=-1, keepdims=True)
            var = jnp.mean(jnp.square(h - mu), axis=-1, keepdims=True)
            return (h - mu) * jax.lax.rsqrt(var + LN_EPS) * g + b

        def _forward_fourier(x, w1, w2):
            xt = jnp.transpose(x, (0, 3, 1, 2))
            B, I, M, N = xt.shape
            nm = w1.shape[2]
            cw1 = w1[..., 0] + 1j * w1[..., 1]
            cw2 = w2[..., 0] + 1j * w2[..., 1]
            O = cw1.shape[1]
            fty = jnp.fft.rfft(xt, axis=-1, norm='ortho')
            f1 = jnp.einsum('bixy,ioy->boxy', fty[..., :nm], cw1)
            pad_y = jnp.zeros((B, O, M, N // 2 + 1 - nm), dtype=f1.dtype)
            xy = jnp.fft.irfft(jnp.concatenate([f1, pad_y], axis=-1), n=N, axis=-1, norm='ortho')
            ftx = jnp.fft.rfft(xt, axis=-2, norm='ortho')
            f2 = jnp.einsum('bixy,iox->boxy', ftx[:, :, :nm, :], cw2)
            pad_x = jnp.zeros((B, O, M // 2 + 1 - nm, N), dtype=f2.dtype)
            xx = jnp.fft.irfft(jnp.concatenate([f2, pad_x], axis=-2), n=M, axis=-2, norm='ortho')
            return jnp.transpose(xx + xy, (0, 2, 3, 1))
        h = _forward_fourier(x, w1, w2)
        h1 = jax.nn.relu(jnp.einsum('bmni,ih->bmnh', h, ff_w0) + ff_b0)
        h2 = jnp.einsum('bmnh,ho->bmno', h1, ff_w1) + ff_b1
        return _layer_norm(h2, ln_g, ln_b)

    def _L2_conv_ref(x, w1, b1, w2, b2):
        import jax, jax.numpy as jnp
        import numpy as np
        from jax import lax
        DN = ('NHWC', 'HWIO', 'NHWC')
        H, W = (x.shape[1], x.shape[2])
        relu = jax.nn.relu

        def c1(t):
            return lax.conv_general_dilated(t, w1, (1, 1), 'SAME', dimension_numbers=DN) + b1
        w2c = w2[0, 4]

        def c2(t):
            return jnp.einsum('bhwc,cd->bhwd', t, w2c) + b2
        t = relu(c1(x))
        y = jnp.concatenate([x[:, :1], x[:, 1:] + t[:, :-1]], axis=1)
        u = relu(c1(y))
        z_main = u + jnp.roll(y, 1, axis=1)
        z = jnp.concatenate([z_main[:, :H - 2], u[:, H - 1:H] + y[:, H - 2:H - 1], y[:, H - 1:H]], axis=1)
        v = relu(c2(z))
        p = jnp.concatenate([z[:, :, :1], z[:, :, 1:] + v[:, :, :-1]], axis=2)
        r = relu(c2(p))
        q_main = r + jnp.roll(p, 1, axis=2)
        q = jnp.concatenate([q_main[:, :, :W - 2], r[:, :, W - 1:W] + p[:, :, W - 2:W - 1], p[:, :, W - 1:W]], axis=2)
        return q

    def _L3_conv_ref(x, A_kernel, B_kernel, gate_A_kernel, gate_B_kernel, W_out, b_out, T):
        import jax, jax.numpy as jnp
        import numpy as np
        EPS = 1e-06

        def kernel_to_freq_2d(kernel, H, W):
            C, kh, kw = kernel.shape
            th = (jnp.arange(kh) - kh // 2) % H
            tw = (jnp.arange(kw) - kw // 2) % W
            TH, TW = jnp.meshgrid(th, tw, indexing='ij')
            padded = jnp.zeros((C, H, W), dtype=kernel.dtype).at[:, TH, TW].set(kernel)
            return jnp.fft.fft2(padded, axes=(1, 2))

        def heinsen_scan_log(log_coeffs, log_values):

            def op(left, right):
                la, lb = left
                ra, rb = right
                return (la + ra, jnp.logaddexp(ra + lb, rb))
            _, log_h = jax.lax.associative_scan(op, (log_coeffs, log_values), axis=0)
            return log_h
        B, H, W, C = x.shape

        def ifft_real(z_bhwc):
            return jnp.fft.ifft2(z_bhwc.transpose(0, 3, 1, 2), axes=(2, 3)).real.transpose(0, 2, 3, 1)
        A_f = kernel_to_freq_2d(A_kernel, H, W).transpose(1, 2, 0)
        B_f = kernel_to_freq_2d(B_kernel, H, W).transpose(1, 2, 0)
        gA_f = kernel_to_freq_2d(gate_A_kernel, H, W).transpose(1, 2, 0)
        gB_f = kernel_to_freq_2d(gate_B_kernel, H, W).transpose(1, 2, 0)
        x_f = jnp.fft.fft2(x.transpose(0, 3, 1, 2), axes=(2, 3)).transpose(0, 2, 3, 1)
        gate_A = jax.nn.sigmoid(ifft_real(gA_f[None] * x_f))
        gate_B = jax.nn.sigmoid(ifft_real(gB_f[None] * x_f))
        a_spatial = ifft_real(jnp.broadcast_to(A_f[None], (B, H, W, C)))
        b_spatial = ifft_real(B_f[None] * x_f)
        a_t = a_spatial * gate_A
        b_t = b_spatial * gate_B
        gate_seq = jnp.tile(a_t[None], (T, 1, 1, 1, 1))
        h_tilde_seq = jnp.tile(b_t[None], (T, 1, 1, 1, 1))
        log_z = -jax.nn.softplus(-gate_seq)
        log_coeffs = -jax.nn.softplus(gate_seq)
        log_values = log_z + jnp.log(jax.nn.softplus(h_tilde_seq) + EPS)
        log_h = heinsen_scan_log(log_coeffs, log_values)
        h_final = jnp.exp(log_h[-1])
        return h_final @ W_out + b_out

    def _gn(v, G=32, eps=1e-5):
        B_, H_, W_, C_ = v.shape
        g = v.reshape(B_, H_, W_, G, C_ // G)
        m = jnp.mean(g, axis=(1, 2, 4), keepdims=True)
        s = jnp.var(g, axis=(1, 2, 4), keepdims=True)
        return ((g - m) / jnp.sqrt(s + eps)).reshape(v.shape)

    def _ln_c(v, eps=1e-6):
        m = jnp.mean(v, axis=-1, keepdims=True)
        s = jnp.var(v, axis=-1, keepdims=True)
        return (v - m) / jnp.sqrt(s + eps)

    def _ln_t(v, eps=1e-5):
        m = jnp.mean(v, axis=-1, keepdims=True)
        s = jnp.var(v, axis=-1, keepdims=True)
        return (v - m) / jnp.sqrt(s + eps)

    def _to_tokens(v):
        B_, H_, W_, C_ = v.shape
        return v.reshape(B_, H_ * W_, C_)
    def _from_tokens(t, like):
        return t.reshape(like.shape)

    x = x + _L0_conv_ref(_gn(x), L0_conv_kv_x, L0_conv_tri_bias, L0_conv_mask_bias, L0_conv_mask, L0_conv_Wq, L0_conv_Wk, L0_conv_Wv, L0_conv_Wg, L0_conv_Wo)
    x = x + _L1_conv_ref(_gn(x), L1_conv_w1, L1_conv_w2, L1_conv_ff_w0, L1_conv_ff_b0, L1_conv_ff_w1, L1_conv_ff_b1, L1_conv_ln_g, L1_conv_ln_b)
    x = x + _L2_conv_ref(_gn(x), L2_conv_w1, L2_conv_b1, L2_conv_w2, L2_conv_b2)
    x = x + _L3_conv_ref(_gn(x), L3_conv_A_kernel, L3_conv_B_kernel, L3_conv_gate_A_kernel, L3_conv_gate_B_kernel, L3_conv_W_out, L3_conv_b_out, 8)
    return x


_drawn_inputs = setup_inputs


def setup_inputs(seed=0):
    import zlib

    import numpy as np

    out = dict(_drawn_inputs(seed))
    spreads = {'L1_conv_ff_b0': (0.0, 0.1),
     'L1_conv_ff_b1': (0.0, 0.1),
     'L1_conv_ln_g': (1.0, 0.2),
     'L1_conv_ln_b': (0.0, 0.1),
     'L2_conv_b2': (0.0, 0.1),
     'L3_conv_b_out': (0.0, 0.1)}
    factors = {'L3_conv_A_kernel': 8.0, 'L3_conv_gate_A_kernel': 8.0, 'L3_conv_gate_B_kernel': 3.802}
    for name, (base, spread) in spreads.items():
        noise = np.random.default_rng([zlib.crc32(name.encode()), seed]).standard_normal(out[name].shape)
        drawn = base * np.exp(spread * noise) if base else spread * noise
        out[name] = jnp.asarray(drawn.astype(out[name].dtype))
    for name, factor in factors.items():
        out[name] = (out[name] * factor).astype(out[name].dtype)
    return out
```

```python
from contextlib import ExitStack

import numpy as np

import concourse.bass as bass
from concourse import mybir

FP32 = mybir.dt.float32
ALU = mybir.AluOpType
ACT = mybir.ActivationFunctionType

ROWS = 256
COLS = 256
CH = 128
TOKENS = ROWS * COLS
HALVES = COLS // 128
BANK = 512
HEADS = 4
HEAD_DIM = CH // HEADS
GN_EPS = 1e-5
EXP_LN_SET = "natural_log_exp_and_others"


class Row:
    BASE = 4

    def __init__(self, q, r=0):
        self.q, self.r = q, r

    def __add__(self, k):
        return type(self)(self.q + (self.r + k) // self.BASE, (self.r + k) % self.BASE)

    @property
    def n(self):
        return self.q * self.BASE + self.r

    def turn(self, ring):
        return self.q * (self.BASE // ring) + self.r // ring


class Tile(Row):
    BASE = 8


class Scope:

    def __init__(self, nc, ctx, phase):
        self.nc, self.ctx, self.phase, self.sems = nc, ctx, phase, []
        ctx.callback(self.end)

    def sb(self, name, shape, dt=FP32):
        return self.ctx.enter_context(self.nc.sbuf_tensor(f"{self.phase}_{name}", shape, dt))

    def ps(self, name, shape):
        return self.ctx.enter_context(self.nc.psum_tensor(f"{self.phase}_{name}", shape, FP32))

    def sem(self, name):
        self.sems.append(self.nc.alloc_semaphore(f"{self.phase}_{name}"))
        return self.sems[-1]

    def end(self):
        self.nc.clear_and_free_semaphores(self.sems)
        self.nc.all_engine_barrier()


def early(n):
    return isinstance(n, int) and n < 2


def in_pairs(eng, count, item):
    for p in range(2):
        item(p, p)
    with eng.Fori(1, count // 2) as i:
        for p in range(2):
            item(i * 2 + p, p)


def uses(n, p):
    return (n - p) // 2 + 1


def pick(view, n):
    return view[n] if isinstance(n, int) else view[bass.ds(n, 1)].squeeze(0)


def input_statistics(nc, x, ident, stats):
    group = 2048
    per, banks, tiles = group // 128, group // BANK, TOKENS // group
    xv = x.rearrange("a h w c -> (a h w) c").rearrange("(t p j) c -> t p (j c)", t=tiles, p=128)
    with ExitStack() as ctx:
        m = Scope(nc, ctx, "in")
        xs = m.sb("xs", [128, 4, per * CH])
        xt = m.ps("xt", [128, 2, banks, BANK])
        loaded = [m.sem(f"loaded{k}") for k in range(4)]
        turned, summed = m.sem("turned"), m.sem("summed")
        block = ctx.enter_context(nc.Block())

        @block.sync
        def _(sp):
            for k in range(4):
                sp.dma_start(xs[:, k, :], xv[k]).then_inc(loaded[k], 16)
            with sp.Fori(1, tiles // 4) as i:
                for k in range(4):
                    sp.wait_ge(turned, i * 4 + (k - 3))
                    sp.dma_start(xs[:, k, :], xv[bass.ds(i * 4 + k, 1)].squeeze(0)).then_inc(loaded[k], 16)

        @block.tensor
        def _(pe):
            def tile(t):
                pe.wait_ge(loaded[t.r], t.q * 16 + 16)
                if not early(t.n):
                    pe.wait_ge(summed, t.n - 1)
                for j in range(per):
                    mm = pe.transpose(xt[:, t.r % 2, j * 128 // BANK, j * 128 % BANK:j * 128 % BANK + 128],
                                      xs[:, t.r, j * CH:(j + 1) * CH], ident[:, :])
                mm.then_inc(turned, 1)

            for k in range(4):
                tile(Row(0, k))
            with pe.Fori(1, tiles // 4) as i:
                for k in range(4):
                    tile(Row(i, k))

        @block.vector
        def _(dve):
            with dve.Fori(0, tiles // 2) as i:
                for p in range(2):
                    dve.wait_ge(turned, i * 2 + p + 1)
                    for b in range(banks):
                        st = dve.bn_stats(stats[:, bass.ds((i * 2 + p) * banks + b, 1), :].squeeze(1), xt[:, p, b, :])
                    st.then_inc(summed, 1)


def group_norm_coefficients(nc, name, stats, group_mean, scale, shift, eps=GN_EPS):
    with ExitStack() as ctx:
        m = Scope(nc, ctx, f"{name}_gn")
        mv = m.sb("mv", [128, 2])
        mean = m.sb("mean", [128, 1])
        apart = m.sb("apart", [128, 1])
        apart2 = m.sb("apart2", [128, 1])
        var = m.sb("var", [128, 1])
        std = m.sb("std", [128, 1])
        epsc = m.sb("eps", [128, 1])
        sums = m.ps("sums", [128, 2, BANK])
        dve_step, pe_step, act_step = m.sem("dve_step"), m.sem("pe_step"), m.sem("act_step")
        block = ctx.enter_context(nc.Block())

        @block.vector
        def _(dve):
            dve.memset(epsc[:, :], eps)
            dve.bn_aggr(mv[:, :], stats).then_inc(dve_step, 1)
            dve.wait_ge(pe_step, 1)
            dve.tensor_copy(mean[:, :], sums[:, 0, 0:1]).then_inc(dve_step, 1)
            dve.wait_ge(dve_step, 2)
            dve.tensor_tensor(apart[:, :], mv[:, 0:1], mean[:, :], ALU.subtract).then_inc(dve_step, 1)
            dve.wait_ge(dve_step, 3)
            dve.tensor_tensor(apart2[:, :], apart[:, :], apart[:, :], ALU.mult).then_inc(dve_step, 1)
            dve.wait_ge(pe_step, 2)
            dve.tensor_copy(var[:, :], sums[:, 0, 1:2]).then_inc(dve_step, 1)
            dve.wait_ge(dve_step, 5)
            dve.tensor_tensor(var[:, :], var[:, :], sums[:, 1, 0:1], ALU.add).then_inc(dve_step, 1)
            dve.wait_ge(act_step, 1)
            dve.reciprocal(scale, std[:, :]).then_inc(dve_step, 1)
            dve.wait_ge(dve_step, 7)
            dve.scalar_tensor_tensor(out=shift, in0=mean[:, :], scalar=-1.0, in1=scale,
                                     op0=ALU.mult, op1=ALU.mult)

        @block.tensor
        def _(pe):
            pe.wait_ge(dve_step, 1)
            pe.matmul(sums[:, 0, 0:2], group_mean, mv[:, :], start=True, stop=True).then_inc(pe_step, 1)
            pe.wait_ge(dve_step, 4)
            pe.matmul(sums[:, 1, 0:1], group_mean, apart2[:, :], start=True, stop=True).then_inc(pe_step, 1)

        @block.scalar
        def _(act):
            act.wait_ge(dve_step, 6)
            act.activation(std[:, :], var[:, :], ACT.Sqrt, bias=epsc[:, :]).then_inc(act_step, 1)


POOL_HEADS = ()


def attention(nc, x, kv, tri_bias, mask_bias, wq, wk, wv, wg, wo, ident, scale, shift, x1, rows=ROWS):
    xv, kvv = x[0].rearrange("r (h p) c -> r p h c", p=128), kv[0].rearrange("r (h p) c -> r p h c", p=128)
    x1v = x1.rearrange("r (h p) c -> r p h c", p=128)
    maskv = mask_bias[0].rearrange("r a b k -> r (a b) k")
    with ExitStack() as ctx:
        m = Scope(nc, ctx, "at")
        weights = m.sb("weights", [128, 5, CH])
        wq_s, wk_s, wv_s, wg_s, wo_s = (weights[:, i, :] for i in range(5))
        bias = m.sb("bias", [128, HEADS, HALVES, COLS])
        xs = m.sb("xs", [128, 4, HALVES, CH])
        kvs = m.sb("kvs", [128, 4, HALVES, CH])
        xn = m.sb("xn", [128, COLS])
        kvt = m.sb("kvt", [128, COLS])
        qz = m.sb("qz", [128, 2, HEADS, COLS])
        keys = m.sb("keys", [128, 4, 2, COLS])
        vs = m.sb("vs", [128, 2, HALVES, CH])
        gate_e = m.sb("gate_e", [128, 2, COLS])
        gate_l = m.sb("gate_l", [128, 2, COLS])
        gate = m.sb("gate", [128, 2, COLS])
        neg_s = m.sb("neg_s", [128, 2, HALVES, COLS])
        neg_max = m.sb("neg_max", [128, 2, HEADS * HALVES])
        probs = m.sb("probs", [128, HEADS, HALVES, COLS])
        sums = m.sb("sums", [128, 2, HEADS * HALVES])
        inv = m.sb("inv", [128, 2, HEADS * HALVES])
        probs_t = m.sb("probs_t", [128, HEADS, HALVES, COLS])
        og = m.sb("og", [128, 2, COLS])
        x1s = m.sb("x1s", [128, 2, HALVES, CH])

        p_turn = m.ps("p_turn", [128, 2, HALVES, 128])
        p_qk = m.ps("p_qk", [128, 2, COLS])
        p_vg = m.ps("p_vg", [128, 2, COLS])
        p_s = [m.ps(f"p_s{i}", [128, HALVES, COLS]) for i in range(2)]
        p_t = [m.ps(f"p_t{i}", [128, HALVES, COLS]) for i in range(2)]
        p_o = m.ps("p_o", [128, 2, COLS])

        const_loaded = m.sem("const_loaded")
        padded = m.sem("padded")
        x_loaded = [m.sem(f"x_loaded{i}") for i in range(4)]
        kv_loaded = [m.sem(f"kv_loaded{i}") for i in range(4)]
        mask_loaded = [m.sem(f"mask_loaded{i}") for i in range(4)]
        x1_stored = [m.sem(f"x1_stored{i}") for i in range(2)]
        turned, turn_read = m.sem("turned"), m.sem("turn_read")
        qk_made, q_read, k_read = m.sem("qk_made"), m.sem("q_read"), m.sem("k_read")
        vg_made, vg_read = m.sem("vg_made"), m.sem("vg_read")
        scored, biased = m.sem("scored"), m.sem("biased")
        exped, inverted, normed = m.sem("exped"), m.sem("inverted"), m.sem("normed")
        p_turned, even_read, odd_read = m.sem("p_turned"), m.sem("even_read"), m.sem("odd_read")
        weighed, gate_log, gate_made, gated = m.sem("weighed"), m.sem("gate_log"), m.sem("gate_made"), m.sem("gated")
        out_made, x1_made = m.sem("out_made"), m.sem("x1_made")
        dve_passed, pool_passed, sp_passed = m.sem("dve_passed"), m.sem("pool_passed"), m.sem("sp_passed")
        block = ctx.enter_context(nc.Block())

        def schedule(eng, step):
            step(Row(-1, 2), turn=True, front=False, back=False, out=False)
            step(Row(-1, 3), turn=True, front=True, back=False, out=False)
            step(Row(0, 0), turn=True, front=True, back=True, out=False)
            turns = (rows - 4) // 4
            with eng.Fori(0, turns) as j:
                for r in range(4):
                    step(Row(j, 0) + (r + 1), turn=True, front=True, back=True, out=True)
            for n in range(4 * turns + 1, rows):
                step(Row(n // 4, n % 4), turn=n + 2 < rows, front=n + 1 < rows, back=True, out=True)
            step(Row(rows // 4, 0), turn=False, front=False, back=False, out=True)

        def first(row):
            return isinstance(row.n, int) and row.n == 0

        def take(v, n):
            return v[n] if isinstance(n, int) else v[bass.ds(n, 1)].squeeze(0)

        @block.sync
        def _(sp):
            for i, w in enumerate((wq, wk, wv, wg, wo)):
                sp.dma_start(weights[:, i, :], w).then_inc(const_loaded, 16)

            def load(row):
                slot = row.r
                sp.dma_start(xs[:, slot], take(xv, row.n)).then_inc(x_loaded[slot], 16)
                sp.dma_start(kvs[:, slot], take(kvv, row.n)).then_inc(kv_loaded[slot], 16)

            def load_mask(row):
                slot = row.r
                sp.dma_start(keys[64:65, slot, 0, :], take(maskv, row.n)).then_inc(mask_loaded[slot], 16)
                sp.dma_start(keys[0:1, slot, 1, :], take(maskv, row.n)).then_inc(mask_loaded[slot], 16)

            for n in range(3):
                load(Row(0, n))
            sp.dma_start(bias[:, :], tri_bias[0, 0].rearrange("h (a p) k -> p h a k", p=128)).then_inc(const_loaded, 16)
            sp.wait_ge(padded, 1)
            for n in range(3):
                load_mask(Row(0, n))

            def step(row, turn, front, back, out):
                ahead = row + 3
                more = not isinstance(row.n, int) or ahead.n < rows
                if back and more:
                    if out:
                        sp.wait_ge(turned, ahead.n - 3)
                        sp.sem_inc(sp_passed, 1)
                        sp.wait_ge(x1_made, row.n)
                        sp.sem_inc(sp_passed, 1)
                    load(ahead)
                    if out:
                        sp.wait_ge(scored, row.n * HEADS)
                        sp.sem_inc(sp_passed, 1)
                    load_mask(ahead)
                if out:
                    prev = row + (-1)
                    sp.wait_ge(x1_made, row.n)
                    sp.dma_start(take(x1v, prev.n), x1s[:, prev.r % 2]).then_inc(x1_stored[prev.r % 2], 16)

            schedule(sp, step)
            for p in range(2):
                sp.wait_ge(x1_stored[p], 16 * (rows // 2))

        @block.tensor
        def _(pe):
            pe.wait_ge(const_loaded, 16 * 6)
            pe.wait_ge(padded, 4)

            def turn_probs(row, h):
                pe.wait_ge(normed, row.n * HEADS + h + 1)
                pe.wait_ge((even_read, odd_read)[h % 2], row.n * 2 + h // 2)
                for kh in range(HALVES):
                    for qh in range(HALVES):
                        mm = pe.transpose(p_t[h % 2][:, kh, qh * 128:(qh + 1) * 128],
                                          probs[:, h, qh, kh * 128:(kh + 1) * 128], ident[:, :])
                mm.then_inc(p_turned, 1)

            def weigh(row, h):
                pe.wait_ge((even_read, odd_read)[h % 2], row.n * 2 + h // 2 + 1)
                ch = slice(HEAD_DIM * h, HEAD_DIM * (h + 1))
                for kh in range(HALVES):
                    mm = pe.matmul(p_o[ch, 0, :], vs[:, row.r % 2, kh, ch], probs_t[:, h, kh, :],
                                   start=kh == 0, stop=kh == HALVES - 1)
                return mm

            def score(row, h):
                if h == 0:
                    pe.wait_ge(q_read, row.n + 1)
                    pe.wait_ge(k_read, row.n + 1)
                    pe.wait_ge(mask_loaded[row.r], 32 * (row.q + 1))
                if h or not first(row):
                    pe.wait_ge(biased, row.n * HEADS + h - 1)
                for qh in range(HALVES):
                    mm = pe.matmul(p_s[h % 2][:, qh, :], qz[:, row.r % 2, h, qh * 128:(qh + 1) * 128],
                                   keys[:, row.r, h // 2, :], start=True, stop=True)
                mm.then_inc(scored, 1)

            def step(row, turn, front, back, out):
                nxt, two = row + 1, row + 2
                if back:
                    turn_probs(row, 0)
                    turn_probs(row, 1)
                if front:
                    score(nxt, 0)
                if out:
                    prev = row + (-1)
                    pe.wait_ge(gated, row.n)
                    for half in range(HALVES):
                        mm = pe.matmul(p_o[:, 1, half * 128:(half + 1) * 128],
                                       og[:, prev.r % 2, half * 128:(half + 1) * 128], wo_s, start=True, stop=True)
                    mm.then_inc(out_made, 1)
                if front:
                    score(nxt, 1)
                    pe.wait_ge(vg_read, nxt.n)
                    for half in range(HALVES):
                        pe.matmul(p_vg[:, 0, half * 128:(half + 1) * 128], kvt[:, half * 128:(half + 1) * 128],
                                  wv_s, start=True, stop=True)
                    pe.matmul(p_vg[:, 1, :], wg_s, xn[:, :], start=True, stop=True).then_inc(vg_made, 1)
                if turn:
                    pe.wait_ge(x_loaded[two.r], 16 * (two.q + 1))
                    pe.wait_ge(kv_loaded[two.r], 16 * (two.q + 1))
                    pe.wait_ge(turn_read, two.n)
                    for i, src in enumerate((xs, kvs)):
                        for half in range(HALVES):
                            mm = pe.transpose(p_turn[:, i, half, :], src[:, two.r, half, :], ident[:, :])
                    mm.then_inc(turned, 1)
                if back:
                    turn_probs(row, 2)
                    pe.wait_ge(x1_made, row.n)
                    weigh(row, 0)
                if front:
                    score(nxt, 2)
                if back:
                    turn_probs(row, 3)
                if turn:
                    pe.wait_ge(turn_read, two.n + 1)
                    pe.wait_ge(q_read, two.n)
                    pe.wait_ge(k_read, two.n)
                    pe.matmul(p_qk[:, 0, :], wq_s, xn[:, :], start=True, stop=True)
                    pe.matmul(p_qk[:, 1, :], wk_s, kvt[:, :], start=True, stop=True).then_inc(qk_made, 1)
                if back:
                    weigh(row, 1)
                if front:
                    score(nxt, 3)
                if back:
                    weigh(row, 2)
                    weigh(row, 3).then_inc(weighed, 1)

            schedule(pe, step)

        @block.scalar
        def _(act):
            act.preload_act_table_set(EXP_LN_SET)

            def read_probs(row, h):
                act.wait_ge(p_turned, row.n * HEADS + h + 1)
                act.activation(probs_t[:, h], p_t[h % 2][:, :, :], ACT.Copy).then_inc(odd_read, 1)

            def exps(row, h):
                act.wait_ge(biased, row.n * HEADS + h + 1)
                for qh in range(HALVES):
                    i = h * HALVES + qh
                    e = act.activation(probs[:, h, qh, :], neg_s[:, h % 2, qh, :], ACT.Exp,
                                       bias=neg_max[:, row.r % 2, i:i + 1], scale=-1.0,
                                       accum_out=sums[:, row.r % 2, i:i + 1])
                e.then_inc(exped, 1)

            def step(row, turn, front, back, out):
                nxt, two = row + 1, row + 2
                p = nxt.r % 2
                if back:
                    read_probs(row, 1)
                if front:
                    exps(nxt, 0)
                    act.wait_ge(vg_made, nxt.n + 1)
                    act.activation(vs[:, p], p_vg[:, 0, :], ACT.Copy)
                    act.activation(gate_e[:, p, :], p_vg[:, 1, :], ACT.Exp, scale=-1.0).then_inc(vg_read, 1)
                    exps(nxt, 1)
                    act.wait_ge(vg_read, nxt.n + 1)
                    act.activation(gate_l[:, p, :], gate_e[:, p, :], ACT.Ln, bias=1.0).then_inc(gate_log, 1)
                if back:
                    read_probs(row, 3)
                if turn:
                    act.wait_ge(qk_made, two.n + 1)
                    for h in range(HEADS):
                        ch = slice(HEAD_DIM * h, HEAD_DIM * (h + 1))
                        t = act.activation(qz[ch, two.r % 2, h, :], p_qk[ch, 0, :], ACT.Copy, scale=float(HEAD_DIM) ** -0.5)
                    t.then_inc(q_read, 1)
                    act.activation(keys[0:64, two.r, 0, :], p_qk[0:64, 1, :], ACT.Copy)
                    act.activation(keys[64:128, two.r, 1, :], p_qk[64:128, 1, :], ACT.Copy).then_inc(k_read, 1)
                if front:
                    exps(nxt, 2)
                    exps(nxt, 3)
                    if not isinstance(nxt.n, int) or nxt.n >= 2:
                        act.wait_ge(gated, nxt.n - 1)
                    act.wait_ge(gate_log, nxt.n + 1)
                    act.activation(gate[:, p, :], gate_l[:, p, :], ACT.Exp, scale=-1.0).then_inc(gate_made, 1)

            schedule(act, step)

        @block.vector
        def _(dve):
            def read_probs(row, h):
                dve.wait_ge(p_turned, row.n * HEADS + h + 1)
                dve.tensor_copy(probs_t[:, h], p_t[h % 2][:, :, :]).then_inc(even_read, 1)

            def add_bias(row, h):
                dve.wait_ge(scored, row.n * HEADS + h + 1)
                if h >= 2 or not first(row):
                    dve.wait_ge(exped, row.n * HEADS + h - 1)
                dve.sem_inc(dve_passed, 1)
                for qh in range(HALVES):
                    i = h * HALVES + qh
                    t = dve.tensor_tensor_reduce(neg_s[:, h % 2, qh, :], p_s[h % 2][:, qh, :], bias[:, h, qh, :],
                                                 -1.0, 3.0e38, ALU.add, ALU.min, neg_max[:, row.r % 2, i:i + 1])
                t.then_inc(biased, 1)

            def invert(row, h):
                p, i = row.r % 2, slice(h * HALVES, (h + 1) * HALVES)
                dve.wait_ge(exped, row.n * HEADS + h + 1)
                dve.reciprocal(inv[:, p, i], sums[:, p, i]).then_inc(inverted, 1)
                if h not in POOL_HEADS:
                    dve.wait_ge(inverted, row.n * HEADS + h + 1)
                    for qh in range(HALVES):
                        j = h * HALVES + qh
                        t = dve.tensor_scalar(probs[:, h, qh, :], probs[:, h, qh, :], inv[:, p, j:j + 1], None, ALU.mult)
                    t.then_inc(normed, 1)

            def step(row, turn, front, back, out):
                nxt, two = row + 1, row + 2
                if back:
                    read_probs(row, 0)
                if front:
                    add_bias(nxt, 0)
                if out:
                    prev = row + (-1)
                    dve.wait_ge(out_made, row.n)
                    if not isinstance(row.n, int) or row.n >= 3:
                        dve.wait_ge(x1_stored[prev.r % 2], 16 * prev.turn(2))
                    dve.tensor_tensor(x1s[:, prev.r % 2].rearrange("p h c -> p (h c)"), p_o[:, 1, :],
                                      xs[:, prev.r].rearrange("p h c -> p (h c)"), ALU.add).then_inc(x1_made, 1)
                if front:
                    add_bias(nxt, 1)
                if turn:
                    dve.wait_ge(turned, two.n + 1)
                    dve.tensor_scalar(xn[:, :], p_turn[:, 0, :, :].rearrange("p h w -> p (h w)"), scale, shift,
                                      ALU.mult, ALU.add)
                    dve.tensor_copy(kvt[:, :], p_turn[:, 1, :, :].rearrange("p h w -> p (h w)")).then_inc(turn_read, 1)
                if back:
                    read_probs(row, 2)
                if front:
                    invert(nxt, 0)
                    add_bias(nxt, 2)
                    invert(nxt, 1)
                    add_bias(nxt, 3)
                if back:
                    dve.wait_ge(weighed, row.n + 1)
                    dve.wait_ge(gate_made, row.n + 1)
                    dve.tensor_tensor(og[:, row.r % 2, :], p_o[:, 0, :], gate[:, row.r % 2, :], ALU.mult).then_inc(gated, 1)
                if front:
                    invert(nxt, 2)
                    invert(nxt, 3)

            schedule(dve, step)

        @block.gpsimd
        def _(pool):
            pool.memset(keys[:, :], 0.0).then_inc(padded, 1)
            pool.memset(qz[:, :], 0.0).then_inc(padded, 1)
            pool.wait_ge(padded, 2)
            pool.memset(qz[64:65, :, 0:2, :], 1.0).then_inc(padded, 1)
            pool.memset(qz[0:1, :, 2:4, :], 1.0).then_inc(padded, 1)

            def step(row, turn, front, back, out):
                nxt = row + 1
                p = nxt.r % 2
                if front:
                    for h in POOL_HEADS:
                        pool.wait_ge(inverted, nxt.n * HEADS + h + 1)
                        pool.sem_inc(pool_passed, 1)
                        for qh in range(HALVES):
                            i = h * HALVES + qh
                            t = pool.tensor_scalar(probs[:, h, qh, :], probs[:, h, qh, :], inv[:, p, i:i + 1],
                                                   None, ALU.mult)
                        t.then_inc(normed, 1)

            schedule(pool, step)


MODES = 16
PARTS = 2 * MODES
HIDDEN = 512
LN_EPS = 1e-5


def spectra(nc, x1, forward, ident, stats, spec):
    tiles = ROWS // 4
    views = (x1.rearrange("(t r) (h p) c -> t p h r c", r=4, p=128),
             x1.rearrange("(h p) (t r) c -> t p h r c", r=4, p=128))
    with ExitStack() as ctx:
        m = Scope(nc, ctx, "sp")
        fwd = m.sb("fwd", [128, HALVES, PARTS])
        xs = m.sb("xs", [128, 4, HALVES, 4, CH])
        out = m.sb("out", [PARTS, 2, 4 * CH])
        p_modes = [m.ps(f"p_modes{p}", [PARTS, 4 * CH]) for p in range(2)]
        p_turn = m.ps("p_turn", [128, 2, HALVES, BANK])
        fwd_loaded = m.sem("fwd_loaded")
        loaded = [m.sem(f"loaded{k}") for k in range(4)]
        stored = [m.sem(f"stored{p}") for p in range(2)]
        made, read, turned, summed = m.sem("made"), m.sem("read"), m.sem("turned"), m.sem("summed")
        block = ctx.enter_context(nc.Block())

        def schedule(eng, item):
            for axis in range(2):
                for k in range(4):
                    item(axis, Row(0, k), axis * tiles + k)
                with eng.Fori(1, tiles // 4) as i:
                    for k in range(4):
                        item(axis, Row(i, k), i * 4 + (axis * tiles + k))

        def known(n, below):
            return isinstance(n, int) and n < below

        @block.sync
        def _(sp):
            sp.dma_start(fwd[:, :, :], forward.rearrange("(h p) k -> p h k", p=128)).then_inc(fwd_loaded, 16)

            def load(axis, t, n):
                if not known(n, 4):
                    sp.wait_ge(made, n - 3)
                for half in range(HALVES):
                    sp.dma_start(xs[:, t.r, half], pick(views[axis], t.n)[:, half]).then_inc(loaded[t.r], 16)

            schedule(sp, load)

        @block.tensor
        def _(pe):
            pe.wait_ge(fwd_loaded, 16)

            def item(axis, t, n):
                p = t.r % 2
                pe.wait_ge(loaded[t.r], t.q * 32 + (axis * tiles // 4 * 32 + 32))
                if axis == 0:
                    if not known(n, 2):
                        pe.wait_ge(summed, n - 1)
                    for r in range(4):
                        for half in range(HALVES):
                            b = r * HALVES + half
                            mm = pe.transpose(p_turn[:, p, b // 4, b % 4 * 128:b % 4 * 128 + 128],
                                              xs[:, t.r, half, r, :], ident[:, :])
                    mm.then_inc(turned, 1)
                if not known(n, 2):
                    pe.wait_ge(read, n - 1)
                for half in range(HALVES):
                    mm = pe.matmul(p_modes[p][:, :], fwd[:, half, :], xs[:, t.r, half].rearrange("p r c -> p (r c)"),
                                   start=half == 0, stop=half == HALVES - 1)
                mm.then_inc(made, 1)

            schedule(pe, item)

        @block.scalar
        def _(act):
            def item(axis, t, n):
                p = t.r % 2
                act.wait_ge(made, n + 1)
                if not known(n, 2):
                    act.wait_ge(stored[p], (t.turn(2) + axis * tiles // 2) * 16)
                act.activation(out[:, p, :], p_modes[p][:, :], ACT.Copy).then_inc(read, 1)
                act.wait_ge(read, n + 1)
                dst = spec[axis].rearrange("k (t r) c -> t k (r c)", r=4)
                act.dma_start(pick(dst, t.n), out[:, p, :]).then_inc(stored[p], 16)

            schedule(act, item)
            for p in range(2):
                act.wait_ge(stored[p], 16 * tiles)

        @block.vector
        def _(dve):
            with dve.Fori(0, tiles // 2) as i:
                for p in range(2):
                    dve.wait_ge(turned, i * 2 + p + 1)
                    for b in range(HALVES):
                        st = dve.bn_stats(stats[:, bass.ds((i * 2 + p) * HALVES + b, 1), :].squeeze(1), p_turn[:, p, b, :])
                    st.then_inc(summed, 1)


def mix_modes(nc, spec, weights, ident, scale, shift, mixed):
    with ExitStack() as ctx:
        m = Scope(nc, ctx, "mx")
        w = m.sb("w", [128, 2, CH, MODES, 2])
        wcat = m.sb("wcat", [128, 2, MODES, 3, CH])
        fs = m.sb("fs", [128, 2, 2, HALVES, CH])
        ft = m.sb("ft", [128, 2, 2, COLS])
        gs = m.sb("gs", [128, 2, HALVES, 2, CH])
        shift0 = m.sb("shift0", [128, 1])
        p_turn = [m.ps(f"p_turn{p}", [128, 2, HALVES, 128]) for p in range(2)]
        p_mix = [m.ps(f"p_mix{p}", [128, HALVES, 2, CH]) for p in range(2)]
        w_loaded, w_split, shifted = m.sem("w_loaded"), m.sem("w_split"), m.sem("shifted")
        loaded = [m.sem(f"loaded{p}") for p in range(2)]
        stored = [m.sem(f"stored{p}") for p in range(2)]
        turned, normed, made, read = m.sem("turned"), m.sem("normed"), m.sem("made"), m.sem("read")
        block = ctx.enter_context(nc.Block())

        def schedule(eng, item):
            for axis in range(2):
                for p in range(2):
                    item(axis, p, p, axis * MODES // 2, axis * MODES + p)
                with eng.Fori(1, MODES // 2) as i:
                    for p in range(2):
                        item(axis, i * 2 + p, p, i + axis * MODES // 2, i * 2 + (axis * MODES + p))

        @block.sync
        def _(sp):
            for axis in range(2):
                sp.dma_start(w[:, axis], weights[axis]).then_inc(w_loaded, 16)

            def load(axis, k, p, use, n):
                if not (isinstance(n, int) and n < 2):
                    sp.wait_ge(turned, n - 1)
                src = spec[axis].rearrange("(k z) (h p) c -> k p z h c", z=2, p=128)
                src = src[k] if isinstance(k, int) else src[bass.ds(k, 1)].squeeze(0)
                for z in range(2):
                    sp.dma_start(fs[:, p, z], src[:, z]).then_inc(loaded[p], 16)

            schedule(sp, load)

        @block.gpsimd
        def _(pool):
            def store(axis, k, p, use, n):
                pool.wait_ge(read, n + 1)
                dst = mixed[axis].rearrange("(h p) (k z) c -> k p h z c", z=2, p=128)
                dst = dst[k] if isinstance(k, int) else dst[bass.ds(k, 1)].squeeze(0)
                for half in range(HALVES):
                    pool.dma_start(dst[:, half], gs[:, p, half]).then_inc(stored[p], 16)

            schedule(pool, store)
            for p in range(2):
                pool.wait_ge(stored[p], 32 * MODES)

        @block.tensor
        def _(pe):
            def item(axis, k, p, use, n):
                pe.wait_ge(loaded[p], use * 32 + 32)
                if not (isinstance(n, int) and n < 2):
                    pe.wait_ge(normed, n - 1)
                for z in range(2):
                    for half in range(HALVES):
                        mm = pe.transpose(p_turn[p][:, z, half, :], fs[:, p, z, half, :], ident[:, :])
                mm.then_inc(turned, 1)
                if isinstance(n, int):
                    pe.wait_ge(w_split, 2 * axis + 2)
                pe.wait_ge(normed, n + 1)
                if not (isinstance(n, int) and n < 2):
                    pe.wait_ge(read, n - 1)
                for half in range(HALVES):
                    for z in range(2):
                        kk = slice(k, k + 1) if isinstance(k, int) else bass.ds(k, 1)
                        mm = pe.matmul(p_mix[p][:, half].rearrange("p z c -> p (z c)"),
                                       ft[:, p, z, half * 128:(half + 1) * 128],
                                       wcat[:, axis, kk, 1 - z:3 - z, :].rearrange("p k z c -> p (k z c)"),
                                       start=z == 0, stop=z == 1)
                mm.then_inc(made, 1)

            schedule(pe, item)

        @block.scalar
        def _(act):
            act.preload_act_table_set(EXP_LN_SET)
            act.activation(shift0[:, :], shift, ACT.Copy, scale=float(COLS) ** 0.5).then_inc(shifted, 1)
            act.wait_ge(shifted, 1)

            def item(axis, k, p, use, n):
                act.wait_ge(turned, n + 1)
                constant = isinstance(k, int) and k == 0
                act.activation(ft[:, p, 0, :], p_turn[p][:, 0], ACT.Identity, scale=scale,
                               bias=shift0[:, :] if constant else 0.0)
                act.activation(ft[:, p, 1, :], p_turn[p][:, 1], ACT.Copy, scale=scale).then_inc(normed, 1)

            schedule(act, item)

        @block.vector
        def _(dve):
            dve.wait_ge(w_loaded, 32)
            for axis in range(2):
                by_mode = w[:, axis].rearrange("p o k z -> p z k o")
                dve.tensor_scalar(wcat[:, axis, :, 0, :], by_mode[:, 1], -1.0, None, ALU.mult)
                dve.tensor_copy(wcat[:, axis, :, 1, :], by_mode[:, 0]).then_inc(w_split, 1)
                dve.tensor_copy(wcat[:, axis, :, 2, :], by_mode[:, 1]).then_inc(w_split, 1)

            def item(axis, k, p, use, n):
                dve.wait_ge(made, n + 1)
                if not (isinstance(n, int) and n < 2):
                    dve.wait_ge(stored[p], use * 32)
                dve.tensor_copy(gs[:, p], p_mix[p][:, :, :, :]).then_inc(read, 1)

            schedule(dve, item)


def waves_along_rows(nc, number, mixed, inverse4, waves):
    quads, ahead = COLS // 4, 8
    with ExitStack() as ctx:
        m = Scope(nc, ctx, f"wr{number}")
        inv = m.sb("inv", [128, 4, 128])
        fs = m.sb("fs", [128, 2, ahead, CH])
        p_w = [m.ps(f"p_w{b}", [128, 4, 128]) for b in range(8)]
        inv_loaded = m.sem("inv_loaded")
        loaded = [m.sem(f"loaded{p}") for p in range(2)]
        made, even_read, odd_read = m.sem("made"), m.sem("even_read"), m.sem("odd_read")
        block = ctx.enter_context(nc.Block())
        chunks = quads // ahead
        view = mixed.rearrange("n k c -> (n k) c").rearrange("(t q p) c -> t p q c", q=ahead, p=128)

        @block.sync
        def _(sp):
            sp.dma_start(inv[:, :, :], inverse4).then_inc(inv_loaded, 16)

            def load(t, p):
                if not early(t):
                    sp.wait_ge(made, (t - 1) * ahead)
                sp.dma_start(fs[:, p], pick(view, t)).then_inc(loaded[p], 16)

            in_pairs(sp, chunks, load)

        @block.tensor
        def _(pe):
            pe.wait_ge(inv_loaded, 16)

            def chunk(t, p):
                pe.wait_ge(loaded[p], uses(t, p) * 16)
                for q in range(ahead):
                    if not (isinstance(t, int) and t == 0):
                        pe.wait_ge((even_read, odd_read)[q % 2], (t - 1) * (ahead // 2) + q // 2 + 1)
                    pe.matmul(p_w[q][:, :, :].rearrange("p a b -> p (a b)"), fs[:, p, q, :],
                              inv[:, :, :].rearrange("p a b -> p (a b)"), start=True, stop=True).then_inc(made, 1)

            in_pairs(pe, chunks, chunk)

        def reader(eng, odd, copy, is_read):
            def chunk(t, p):
                for q in range(odd, ahead, 2):
                    eng.wait_ge(made, t * ahead + q + 1)
                    copy(waves[:, :, bass.ds((t * ahead + q) * 4, 4)].rearrange("c r n -> c n r"),
                         p_w[q][:, :, :]).then_inc(is_read, 1)

            in_pairs(eng, chunks, chunk)

        @block.vector
        def _(dve):
            reader(dve, 0, dve.tensor_copy, even_read)

        @block.scalar
        def _(act):
            reader(act, 1, lambda out, in_: act.activation(out, in_, ACT.Copy), odd_read)


def mlp(nc, half, x1, mixed_y, inverse_y, waves, prepared, ident, x2, stats):
    w0, w1c, b0, b1c, ln_g, ln_b, mean_of, eps = prepared
    tiles = ROWS // 2 // HALVES
    first_tile = half * tiles
    blocks = HIDDEN // 128
    x1v = x1[half * 128:(half + 1) * 128].rearrange("(t r) (h p) c -> t p (r h) c", r=2, p=128)
    quadv = mixed_y[half * 128:(half + 1) * 128].rearrange("n k c -> (n k) c").rearrange("(t p) c -> t p c", p=128)
    with ExitStack() as ctx:
        m = Scope(nc, ctx, f"ml{half}")
        inv = m.sb("inv", [128, 2, BANK])
        fs = m.sb("fs", [128, 2, CH])
        xs = m.sb("xs", [128, 2, 4, CH])
        xb = m.sb("xb", [128, 2, BANK])
        h = m.sb("h", [128, BANK])
        h1 = m.sb("h1", [128, blocks, BANK])
        sq = m.sb("sq", [128, BANK])
        logv = m.sb("logv", [128, BANK])
        rstd = m.sb("rstd", [128, BANK])
        normed = m.sb("normed", [128, BANK])
        x2s = m.sb("x2s", [128, 2, BANK])
        p_h = m.ps("p_h", [128, BANK])
        p_1 = [m.ps(f"p_1{b}", [128, BANK]) for b in range(blocks)]
        p_2 = m.ps("p_2", [128, BANK])
        p_var = m.ps("p_var", [128, BANK])
        p_x = m.ps("p_x", [128, 4, 128])
        inv_loaded = m.sem("inv_loaded")
        x_loaded = [m.sem(f"x_loaded{p}") for p in range(2)]
        f_loaded = [m.sem(f"f_loaded{p}") for p in range(2)]
        stored = [m.sem(f"stored{p}") for p in range(2)]
        inverted, summed, hid_made = m.sem("inverted"), m.sem("summed"), m.sem("hid_made")
        relu_act, relu_dve = m.sem("relu_act"), m.sem("relu_dve")
        second, squared, var_made, logged, rooted = (m.sem(x) for x in ("second", "squared", "var_made", "logged", "rooted"))
        x_turned, x_biased, normal, added, counted = (m.sem(x) for x in ("x_turned", "x_biased", "normal", "added", "counted"))
        block = ctx.enter_context(nc.Block())
        by_dve = 1

        def schedule(eng, step):
            for t in range(4):
                step(Row(0, t))
            with eng.Fori(1, tiles // 4) as i:
                for r in range(4):
                    step(Row(i, r))

        def known(t, below):
            return isinstance(t.n, int) and t.n < below

        @block.sync
        def _(sp):
            sp.dma_start(inv[:, :, :], inverse_y).then_inc(inv_loaded, 16)

            def step(t):
                p, quad = t.r % 2, t.r // 2
                if p == 0:
                    if not known(t, 4):
                        sp.wait_ge(inverted, t.n - 2)
                    sp.dma_start(fs[:, quad, :], pick(quadv, t.q * 2 + quad)).then_inc(f_loaded[quad], 16)
                if not known(t, 2):
                    sp.wait_ge(x_turned, t.n - 1)
                sp.dma_start(xs[:, p], pick(x1v, t.n)).then_inc(x_loaded[p], 16)

            schedule(sp, step)

        @block.gpsimd
        def _(pool):
            def step(t):
                pool.wait_ge(added, t.n + 1)
                dst = x2[:, bass.ds((t.n + first_tile) * BANK, BANK)]
                pool.dma_start(dst, x2s[:, t.r % 2, :]).then_inc(stored[t.r % 2], 16)

            schedule(pool, step)
            for p in range(2):
                pool.wait_ge(stored[p], 16 * tiles // 2)

        @block.tensor
        def _(pe):
            def invert(t):
                quad = t.r // 2
                if t.r % 2 == 0:
                    pe.wait_ge(f_loaded[quad], t.q * 16 + 16)
                pe.wait_ge(summed, t.n)
                pe.matmul(p_h[:, :], fs[:, quad, :], inv[:, t.r % 2, :], start=True, stop=True).then_inc(inverted, 1)

            def variance(t):
                pe.wait_ge(squared, t.n + 1)
                if not known(t, 1):
                    pe.wait_ge(logged, t.n)
                pe.matmul(p_var[:, :], mean_of, sq[:, :], start=True, stop=True).then_inc(var_made, 1)

            def step(t, last=False):
                for b in range(blocks):
                    if b == 0:
                        pe.wait_ge(summed, t.n + 1)
                    if not known(t, 1):
                        if b < by_dve:
                            pe.wait_ge(relu_dve, t.n * by_dve - by_dve + b + 1)
                        else:
                            pe.wait_ge(relu_act, t.n * (blocks - by_dve) - blocks + b + 1)
                    pe.matmul(p_1[b][:, :], w0[:, b * 128:(b + 1) * 128], h[:, :], start=True, stop=True).then_inc(hid_made, 1)
                    if b == 0 and not known(t, 1):
                        variance(t + (-1))
                if not last:
                    invert(t + 1)
                pe.wait_ge(x_loaded[t.r % 2], t.turn(2) * 16 + 16)
                pe.wait_ge(x_biased, t.n)
                for j in range(4):
                    mm = pe.transpose(p_x[:, j, :], xs[:, t.r % 2, j, :], ident[:, :])
                mm.then_inc(x_turned, 1)
                pe.wait_ge(normal, t.n)
                for b in range(blocks):
                    if b < by_dve:
                        pe.wait_ge(relu_dve, t.n * by_dve + b + 1)
                    else:
                        pe.wait_ge(relu_act, t.n * (blocks - by_dve) + b - by_dve + 1)
                    mm = pe.matmul(p_2[:, :], w1c[:, b, :], h1[:, b, :], start=b == 0, stop=b == blocks - 1)
                mm.then_inc(second, 1)

            pe.wait_ge(inv_loaded, 16)
            invert(Row(0, 0))
            for t in range(4):
                step(Row(0, t))
            with pe.Fori(1, tiles // 4 - 1) as i:
                for r in range(4):
                    step(Row(i, r))
            for t in range(tiles - 4, tiles):
                step(Row(t // 4, t % 4), last=t == tiles - 1)
            variance(Row((tiles - 1) // 4, (tiles - 1) % 4))

        @block.scalar
        def _(act):
            act.preload_act_table_set(EXP_LN_SET)

            def finish(t):
                act.wait_ge(var_made, t.n + 1)
                act.activation(logv[:, :], p_var[:, :], ACT.Ln, bias=eps).then_inc(logged, 1)
                act.wait_ge(logged, t.n + 1)
                act.wait_ge(normal, t.n)
                act.activation(rstd[:, :], logv[:, :], ACT.Exp, scale=-0.5).then_inc(rooted, 1)

            def step(t):
                for b in range(by_dve, blocks):
                    act.wait_ge(hid_made, t.n * blocks + b + 1)
                    act.wait_ge(second, t.n)
                    act.activation(h1[:, b, :], p_1[b][:, :], ACT.Relu, bias=b0[:, b:b + 1]).then_inc(relu_act, 1)
                    if b == by_dve and not known(t, 1):
                        finish(t + (-1))
                act.wait_ge(x_turned, t.n + 1)
                if not known(t, 2):
                    act.wait_ge(added, t.n - 1)
                act.activation(xb[:, t.r % 2, :], p_x[:, :, :].rearrange("p a b -> p (a b)"), ACT.Identity,
                               bias=ln_b).then_inc(x_biased, 1)
                act.wait_ge(second, t.n + 1)
                act.wait_ge(var_made, t.n)
                act.activation(sq[:, :], p_2[:, :], ACT.Square, bias=b1c).then_inc(squared, 1)

            schedule(act, step)
            finish(Row((tiles - 1) // 4, (tiles - 1) % 4))

        @block.vector
        def _(dve):
            def add_waves(t):
                dve.wait_ge(inverted, t.n + 1)
                if not known(t, 1):
                    dve.wait_ge(hid_made, t.n * blocks)
                dve.tensor_tensor(h[:, :].rearrange("p (r n) -> p r n", r=2), p_h[:, :].rearrange("p (r n) -> p r n", r=2),
                                  waves[:, bass.ds(t.n * 2, 2), :], ALU.add).then_inc(summed, 1)

            def finish(t):
                p = t.r % 2
                dve.wait_ge(rooted, t.n + 1)
                if not known(t, 1):
                    dve.wait_ge(added, t.n)
                dve.scalar_tensor_tensor(out=normed[:, :], in0=p_2[:, :], scalar=b1c, in1=rstd[:, :],
                                         op0=ALU.add, op1=ALU.mult).then_inc(normal, 1)
                dve.wait_ge(normal, t.n + 1)
                dve.wait_ge(x_biased, t.n + 1)
                if not known(t, 2):
                    dve.wait_ge(stored[p], t.turn(2) * 16)
                    dve.wait_ge(counted, t.n - 1)
                dve.scalar_tensor_tensor(out=x2s[:, p, :], in0=normed[:, :], scalar=ln_g, in1=xb[:, p, :],
                                         op0=ALU.mult, op1=ALU.add).then_inc(added, 1)
                dve.wait_ge(added, t.n + 1)
                dve.bn_stats(stats[:, bass.ds(t.n + first_tile, 1), :].squeeze(1), x2s[:, p, :]).then_inc(counted, 1)

            def step(t, last=False):
                for b in range(by_dve):
                    dve.wait_ge(hid_made, t.n * blocks + b + 1)
                    dve.wait_ge(second, t.n)
                    dve.tensor_scalar(h1[:, b, :], p_1[b][:, :], b0[:, b:b + 1], 0.0, ALU.add, ALU.max).then_inc(relu_dve, 1)
                if not known(t, 1):
                    finish(t + (-1))
                if not last:
                    add_waves(t + 1)

            add_waves(Row(0, 0))
            for t in range(4):
                step(Row(0, t))
            with dve.Fori(1, tiles // 4 - 1) as i:
                for r in range(4):
                    step(Row(i, r))
            for t in range(tiles - 4, tiles):
                step(Row(t // 4, t % 4), last=t == tiles - 1)
            finish(Row((tiles - 1) // 4, (tiles - 1) % 4))


def fourier_layer(nc, x1, w1, w2, ff_w0, ff_b0, ff_w1, ff_b1, ln_g, ln_b, consts, ident, group_mean, coef,
                  spec, mixed, x2, stats_out):
    fp = FP32
    with ExitStack() as ctx:
        with nc.sbuf_tensor("l1_stats", [128, TOKENS // BANK, 6], fp) as stats:
            spectra(nc, x1, consts["forward"], ident, stats, spec)
            group_norm_coefficients(nc, "l1", stats[:, :, :].rearrange("p a b -> p (a b)"), group_mean,
                                    coef[:, 0:1], coef[:, 1:2])
        mix_modes(nc, spec, (w1, w2), ident, coef[:, 0:1], coef[:, 1:2], mixed)
        m = Scope(nc, ctx, "l1")
        w0 = m.sb("w0", [128, HIDDEN])
        w1s = m.sb("w1s", [128, HIDDEN // 128, CH])
        rows = m.sb("rows", [128, HIDDEN // 128])
        vec = m.sb("vec", [128, 8])
        b1, g, b, b1c, eps = (vec[:, i:i + 1] for i in range(5))
        b0 = m.sb("b0", [128, HIDDEN // 128])
        mean_of = m.sb("mean_of", [128, CH])
        prepare_mlp(nc, ff_w0, ff_b0, ff_w1, ff_b1, ln_g, ln_b, w0, w1s, rows, b0, vec, mean_of)
        waves = m.sb("waves", [128, ROWS // 2, COLS])
        prepared = (w0, w1s, b0, b1c, g, b, mean_of[:, :], eps)
        for half in range(2):
            waves_along_rows(nc, half, mixed[1], consts["inverse_rows"][half], waves)
            mlp(nc, half, x1, mixed[0], consts["inverse_cols"], waves, prepared, ident, x2, stats_out)


def prepare_mlp(nc, ff_w0, ff_b0, ff_w1, ff_b1, ln_g, ln_b, w0, w1s, rows, b0, vec, mean_of):
    blocks = HIDDEN // 128
    b1, b1c, eps = vec[:, 0:1], vec[:, 3:4], vec[:, 4:5]
    with ExitStack() as ctx:
        m = Scope(nc, ctx, "pm")
        p_mean = m.ps("p_mean", [128, 1])
        loaded, step = m.sem("loaded"), m.sem("step")
        mean_made = m.sem("mean_made")
        block = ctx.enter_context(nc.Block())

        @block.sync
        def _(sp):
            sp.dma_start(w0[:, :], ff_w0).then_inc(loaded, 16)
            sp.dma_start(w1s[:, :, :], ff_w1.rearrange("(b p) c -> p b c", p=128)).then_inc(loaded, 16)
            sp.dma_start(b0[:, :], ff_b0.rearrange("(b p) -> p b", p=128), allow_slow_non_contiguous=True).then_inc(loaded, 16)
            for i, v in ((0, ff_b1), (1, ln_g), (2, ln_b)):
                sp.dma_start(vec[:, i:i + 1], v.rearrange("(p a) -> p a", a=1)).then_inc(loaded, 16)

        @block.vector
        def _(dve):
            dve.memset(eps, LN_EPS)
            dve.memset(mean_of[:, :], 1.0 / CH).then_inc(step, 1)
            dve.wait_ge(loaded, 16 * 6)
            dve.tensor_reduce(rows[:, :], w1s[:, :, :], mybir.AxisListType.X, ALU.add).then_inc(step, 1)
            dve.wait_ge(step, 2)
            dve.tensor_scalar(rows[:, :], rows[:, :], 1.0 / CH, None, ALU.mult).then_inc(step, 1)
            dve.wait_ge(step, 3)
            for b in range(blocks):
                dve.tensor_scalar(w1s[:, b, :], w1s[:, b, :], rows[:, b:b + 1], None, ALU.subtract)
            dve.wait_ge(mean_made, 1)
            dve.tensor_tensor(b1c, b1, p_mean[:, :], ALU.subtract)

        @block.tensor
        def _(pe):
            pe.wait_ge(loaded, 16 * 6)
            pe.wait_ge(step, 1)
            pe.matmul(p_mean[:, :], mean_of[:, :], b1, start=True, stop=True).then_inc(mean_made, 1)


TAPS = 9
HALO = 3
PADDED = ROWS + 2 * HALO
PATCH = 8
WINDOW = PATCH + 2 * HALO
PADDED_ROWS = ROWS + PATCH


def row_taps(nc, x2, w1, scale, shift, taps):
    wide = 4 * BANK
    tiles = TOKENS // wide
    with ExitStack() as ctx:
        m = Scope(nc, ctx, "tp")
        w = m.sb("w", [128, TAPS])
        ws = m.sb("ws", [128, TAPS])
        tap_bias = m.sb("tap_bias", [TAPS, 1])
        xs = m.sb("xs", [128, 2, wide])
        out = m.sb("out", [TAPS, 2, wide])
        p_out = [m.ps(f"p_out{p}", [TAPS, wide]) for p in range(2)]
        p_bias = p_out[0][:, 0:1]
        w_loaded, w_scaled = m.sem("w_loaded"), m.sem("w_scaled")
        bias_made, bias_read = m.sem("bias_made"), m.sem("bias_read")
        loaded = [m.sem(f"loaded{p}") for p in range(2)]
        stored = [m.sem(f"stored{p}") for p in range(2)]
        made = m.sem("made")
        read = m.sem("read")
        block = ctx.enter_context(nc.Block())

        @block.sync
        def _(sp):
            sp.dma_start(w[:, :], w1.rearrange("a j c d -> c (a j d)"), allow_slow_non_contiguous=True).then_inc(w_loaded, 16)

            def load(t, p):
                if not early(t):
                    sp.wait_ge(made, t - 1)
                sp.dma_start(xs[:, p], pick(x2.rearrange("c (t n) -> t c n", n=wide), t)).then_inc(loaded[p], 16)

            in_pairs(sp, tiles, load)

        @block.vector
        def _(dve):
            dve.wait_ge(w_loaded, 16)
            dve.tensor_scalar(ws[:, :], w[:, :], scale, None, ALU.mult).then_inc(w_scaled, 1)
            dve.wait_ge(bias_made, 1)
            dve.tensor_copy(tap_bias[:, :], p_bias).then_inc(bias_read, 1)

        @block.tensor
        def _(pe):
            pe.wait_ge(w_loaded, 16)
            pe.matmul(p_bias, w[:, :], shift, start=True, stop=True).then_inc(bias_made, 1)
            pe.wait_ge(w_scaled, 1)
            pe.wait_ge(bias_read, 1)

            def tile(t, p):
                pe.wait_ge(loaded[p], uses(t, p) * 16)
                if not early(t):
                    pe.wait_ge(read, t - 1)
                for b in range(4):
                    mm = pe.matmul(p_out[p][:, b * BANK:(b + 1) * BANK], ws[:, :], xs[:, p, b * BANK:(b + 1) * BANK],
                                   start=True, stop=True)
                mm.then_inc(made, 1)

            in_pairs(pe, tiles, tile)

        @block.scalar
        def _(act):
            act.wait_ge(bias_read, 1)

            def tile(t, p):
                act.wait_ge(made, t + 1)
                if not early(t):
                    act.wait_ge(stored[p], uses(t, p) * 16 - 16)
                act.activation(out[:, p, :], p_out[p][:, :], ACT.Identity, bias=tap_bias[:, :]).then_inc(read, 1)
                act.wait_ge(read, t + 1)
                act.dma_start(pick(taps.rearrange("j (t n) -> t j n", n=wide), t), out[:, p, :]).then_inc(stored[p], 16)

            in_pairs(act, tiles, tile)
            for p in range(2):
                act.wait_ge(stored[p], 16 * (tiles // 2))


def one_channel_part(nc, taps, w1, b1, scratch, tau):
    side = TAPS // 2
    wide = COLS + 2 * side
    t_d, u_d = scratch[0], scratch[1]
    with ExitStack() as ctx:
        m = Scope(nc, ctx, "oc")
        w = m.sb("w", [128, TAPS])
        ones = m.sb("ones", [128, 128])
        tap_sum = m.sb("tap_sum", [128, TAPS])
        b1s = m.sb("b1s", [128, 1])
        ts = m.sb("ts", [128, 2, TAPS, wide])
        acc = m.sb("acc", [128, 2, COLS])
        t = m.sb("t", [128, 2, COLS])
        above = m.sb("above", [128, 2, wide])
        u = m.sb("u", [128, 2, COLS])
        u_of = m.sb("u_of", [128, 2, COLS])
        t_of = m.sb("t_of", [128, 2, COLS])
        p_sum = m.ps("p_sum", [128, TAPS])
        small_loaded, taps_loaded = m.sem("small_loaded"), m.sem("taps_loaded")
        t_stored, u_stored, tau_stored = m.sem("t_stored"), m.sem("u_stored"), m.sem("tau_stored")
        above_loaded, tau_loaded = m.sem("above_loaded"), m.sem("tau_loaded")
        cleared, step, sum_made = m.sem("cleared"), m.sem("step"), m.sem("sum_made")
        t_made, u_made, tau_made = m.sem("t_made"), m.sem("u_made"), m.sem("tau_made")
        block = ctx.enter_context(nc.Block())

        def place(sp, dst, src, first, count, start, done):
            n = 0
            while count:
                k = min(count, 128 - first % 128)
                p, half = first % 128, first // 128
                sp.dma_start(dst[p:p + k, half], src[start:start + k]).then_inc(done, 16)
                first, start, count, n = first + k, start + k, count - k, n + 1
            return n

        @block.sync
        def _(sp):
            sp.dma_start(w[:, :], w1.rearrange("a j c d -> c (a j d)"), allow_slow_non_contiguous=True).then_inc(small_loaded, 16)
            sp.dma_start(b1s[:, :], b1.rearrange("(a n) -> a n", a=1).to_broadcast((128, 1))).then_inc(small_loaded, 16)
            sp.wait_ge(cleared, 4)
            for half in range(2):
                sp.dma_start(ts[:, half, :, side:side + COLS],
                             taps.rearrange("j (h p w) -> h p j w", p=128, w=COLS)[half]).then_inc(taps_loaded, 16)
            sp.wait_ge(t_made, 1)
            sp.dma_start(t_d.rearrange("(h p) w -> p h w", p=128), t[:, :, :]).then_inc(t_stored, 16)
            sp.wait_ge(t_stored, 16)
            place(sp, above[:, :, side:side + COLS], t_d, 1, ROWS - 1, 0, above_loaded)
            n = place(sp, t_of, t_d, 0, 1, ROWS - 2, tau_loaded)
            n += place(sp, t_of, t_d, 2, ROWS - 4, 0, tau_loaded)
            n += place(sp, t_of, t_d, ROWS - 2, 2, ROWS - 3, tau_loaded)
            sp.wait_ge(u_made, 1)
            sp.dma_start(u_d.rearrange("(h p) w -> p h w", p=128), u[:, :, :]).then_inc(u_stored, 16)
            sp.wait_ge(u_stored, 16)
            n += place(sp, u_of, u_d, 0, ROWS - 2, 0, tau_loaded)
            n += place(sp, u_of, u_d, ROWS - 2, 1, ROWS - 1, tau_loaded)
            assert n == 7
            sp.wait_ge(tau_made, 1)
            sp.dma_start(tau.rearrange("(h p w) -> p h w", p=128, w=COLS), u_of[:, :, :]).then_inc(tau_stored, 16)
            sp.wait_ge(tau_stored, 16)

        @block.tensor
        def _(pe):
            pe.wait_ge(small_loaded, 32)
            pe.wait_ge(cleared, 4)
            pe.matmul(p_sum[:, :], ones[:, :], w[:, :], start=True, stop=True).then_inc(sum_made, 1)

        @block.gpsimd
        def _(pool):
            pool.memset(ts[:, :, :, :], 0.0).then_inc(cleared, 1)
            pool.memset(above[:, :, :], 0.0).then_inc(cleared, 1)
            pool.memset(ones[:, :], 1.0).then_inc(cleared, 1)
            pool.memset(u_of[:, :, :], 0.0)
            pool.memset(t_of[:, :, :], 0.0).then_inc(cleared, 1)

        @block.vector
        def _(dve):
            dve.wait_ge(sum_made, 1)
            dve.tensor_copy(tap_sum[:, :], p_sum[:, :]).then_inc(step, 1)
            dve.wait_ge(taps_loaded, 32)
            done = 1
            dve.tensor_scalar(acc[:, :, :], ts[:, :, 0, 0:COLS], b1s[:, :], None, ALU.add).then_inc(step, 1)
            for j in range(1, TAPS):
                done += 1
                dve.wait_ge(step, done)
                dve.tensor_tensor(acc[:, :, :], acc[:, :, :], ts[:, :, j, j:j + COLS], ALU.add).then_inc(step, 1)
            done += 1
            dve.wait_ge(step, done)
            dve.tensor_scalar(t[:, :, :], acc[:, :, :], 0.0, None, ALU.max).then_inc(t_made, 1)
            dve.wait_ge(above_loaded, 32)
            for j in range(TAPS):
                dve.wait_ge(step, done)
                for half in range(2):
                    a = dve.scalar_tensor_tensor(out=acc[:, half], in0=above[:, half, j:j + COLS],
                                                 scalar=tap_sum[:, j:j + 1], in1=acc[:, half], op0=ALU.mult, op1=ALU.add)
                a.then_inc(step, 1)
                done += 1
            dve.wait_ge(step, done)
            dve.tensor_scalar(u[:, :, :], acc[:, :, :], 0.0, None, ALU.max).then_inc(u_made, 1)
            dve.wait_ge(tau_loaded, 16 * 7)
            dve.tensor_tensor(u_of[:, :, :], u_of[:, :, :], t_of[:, :, :], ALU.add).then_inc(tau_made, 1)


def pointwise_part(nc, x2, tau, w2, b2, scale, shift, ident, x3, stats):
    tiles = ROWS // 2
    rows = x2.rearrange("c (r w) -> c r w", w=COLS)
    x3v = x3[HALO:HALO + ROWS, HALO:HALO + COLS].rearrange("(t r) (h p) c -> t p r h c", r=2, p=128)
    with ExitStack() as ctx:
        m = Scope(nc, ctx, "pw")
        w = m.sb("w", [128, CH])
        b2s = m.sb("b2s", [128, 1])
        bias = m.sb("bias", [128, 1])
        xs = m.sb("xs", [128, 8, 3, COLS])
        taus = m.sb("taus", [128, 8, 2, COLS])
        z = m.sb("z", [128, 4, 2, COLS])
        v = m.sb("v", [128, 2, 2, COLS + 1])
        p = m.sb("p", [128, 2, 2, COLS + 1])
        r = m.sb("r", [128, 2, 2, COLS])
        q = m.sb("q", [128, 2, 2, COLS])
        x3s = m.sb("x3s", [128, 2, 2, COLS])
        x3n = m.sb("x3n", [128, 2, 2, HALVES, CH])
        p_v = [m.ps(f"p_v{i}", [128, 2, COLS]) for i in range(2)]
        p_r = [m.ps(f"p_r{i}", [128, 2, COLS]) for i in range(2)]
        p_n = [m.ps(f"p_n{i}", [128, 2, HALVES, 128]) for i in range(2)]
        p_bias = m.ps("p_bias", [128, 1])
        small_loaded, cleared, bias_made, bias_ready = (m.sem(n) for n in ("small_loaded", "cleared", "bias_made", "bias_ready"))
        loaded = [m.sem(f"loaded{i}") for i in range(8)]
        wrap_loaded = m.sem("wrap_loaded")
        stored = [m.sem(f"stored{i}") for i in range(2)]
        z_made, v_mul, v_made, p_made = (m.sem(n) for n in ("z_made", "v_mul", "v_made", "p_made"))
        r_mul, r_made, p_wrapped, q_made = (m.sem(n) for n in ("r_mul", "r_made", "p_wrapped", "q_made"))
        pool_passed = m.sem("pool_passed")
        x3_made, counted, x3_turned, x3_read = (m.sem(n) for n in ("x3_made", "counted", "x3_turned", "x3_read"))
        block = ctx.enter_context(nc.Block())

        def exists(t):
            return not isinstance(t.n, int) or 0 <= t.n < tiles

        def known(t, below):
            return isinstance(t.n, int) and t.n < below

        def schedule(eng, step):
            for t in range(-2, 8):
                step(Tile(t // 8, t % 8))
            with eng.Fori(1, tiles // 8 - 1) as i:
                for k in range(8):
                    step(Tile(i, k))
            for t in range(tiles - 8, tiles + 2):
                step(Tile(t // 8, t % 8))

        @block.sync
        def _(sp):
            sp.dma_start(w[:, :], w2[0, TAPS // 2]).then_inc(small_loaded, 16)
            sp.dma_start(b2s[:, :], b2.rearrange("(p a) -> p a", a=1)).then_inc(small_loaded, 16)

            def load(g):
                slot = g.r
                if not known(g, 8):
                    sp.wait_ge(z_made, g.n - 7)
                    sp.wait_ge(x3_made, g.n - 7)
                if known(g, 1):
                    sp.dma_start(xs[:, slot, 0], rows[:, ROWS - 1]).then_inc(wrap_loaded, 16)
                    sp.dma_start(xs[:, slot, 1:3], rows[:, 0:2]).then_inc(loaded[slot], 16)
                else:
                    sp.dma_start(xs[:, slot], rows[:, bass.ds(g.n * 2 - 1, 3)]).then_inc(loaded[slot], 16)
                t_src = tau.rearrange("(g n) -> g n", n=2 * COLS)
                t_src = t_src[g.n:g.n + 1] if isinstance(g.n, int) else t_src[bass.ds(g.n, 1)]
                sp.dma_start(taus[:, slot].rearrange("p r w -> p (r w)"),
                             t_src.to_broadcast((128, 2 * COLS))).then_inc(loaded[slot], 16)

            for n in range(4):
                load(Tile(0, n))

            def step(t):
                if exists(t + 6):
                    load(t + 6)

            schedule(sp, step)

        @block.gpsimd
        def _(pool):
            pool.memset(v[:, :, :, :], 0.0).then_inc(cleared, 1)

            def step(t):
                if exists(t):
                    s = t.r % 2
                    pool.wait_ge(p_made, t.n + 1)
                    pool.sem_inc(pool_passed, 1)
                    pool.tensor_copy(p[:, s, :, 0:1], p[:, s, :, COLS:COLS + 1]).then_inc(p_wrapped, 1)
                    pool.wait_ge(r_made, t.n + 1)
                    if not known(t, 2):
                        pool.wait_ge(x3_made, t.n - 1)
                    pool.wait_ge(p_wrapped, t.n + 1)
                    pool.tensor_tensor(q[:, s, :, 0:COLS - 2], r[:, s, :, 0:COLS - 2], p[:, s, :, 0:COLS - 2], ALU.add)
                    pool.tensor_tensor(q[:, s, :, COLS - 2:COLS - 1], r[:, s, :, COLS - 1:COLS],
                                       p[:, s, :, COLS - 1:COLS], ALU.add)
                    pool.tensor_copy(q[:, s, :, COLS - 1:COLS], p[:, s, :, COLS:COLS + 1]).then_inc(q_made, 1)

            schedule(pool, step)

        @block.tensor
        def _(pe):
            pe.wait_ge(small_loaded, 32)
            pe.matmul(p_bias[:, :], w[:, :], shift, start=True, stop=True).then_inc(bias_made, 1)

            def step(t):
                a, c = t + 1, t + (-2)
                if exists(a):
                    pe.wait_ge(z_made, a.n + 1)
                    if not known(a, 2):
                        pe.wait_ge(v_made, a.n - 1)
                    pe.matmul(p_v[a.r % 2][:, :, :].rearrange("p r w -> p (r w)"), w[:, :],
                              z[:, a.r % 4].rearrange("p r w -> p (r w)"), start=True, stop=True).then_inc(v_mul, 1)
                if exists(t):
                    pe.wait_ge(p_made, t.n + 1)
                    if not known(t, 2):
                        pe.wait_ge(r_made, t.n - 1)
                    pe.matmul(p_r[t.r % 2][:, :, :], w[:, :], p[:, t.r % 2, :, 1:COLS + 1], start=True, stop=True).then_inc(r_mul, 1)
                if exists(c):
                    s = c.r % 2
                    pe.wait_ge(x3_made, c.n + 1)
                    if not known(c, 2):
                        pe.wait_ge(x3_read, c.n - 1)
                    for row in range(2):
                        for half in range(HALVES):
                            mm = pe.transpose(p_n[s][:, row, half, :], x3s[:, s, row, half * 128:(half + 1) * 128], ident[:, :])
                    mm.then_inc(x3_turned, 1)

            schedule(pe, step)

        @block.scalar
        def _(act):
            act.wait_ge(bias_ready, 1)
            act.wait_ge(cleared, 1)

            def step(t):
                a, c = t + 1, t + (-2)
                if exists(a):
                    s = a.r % 2
                    act.wait_ge(v_mul, a.n + 1)
                    if not known(a, 2):
                        act.wait_ge(p_made, a.n - 1)
                    act.activation(v[:, s, :, 1:COLS + 1], p_v[s][:, :, :], ACT.Relu, bias=bias[:, :]).then_inc(v_made, 1)
                if exists(t):
                    s = t.r % 2
                    act.wait_ge(r_mul, t.n + 1)
                    if not known(t, 2):
                        act.wait_ge(q_made, t.n - 1)
                    act.activation(r[:, s], p_r[s][:, :, :], ACT.Relu, bias=bias[:, :]).then_inc(r_made, 1)
                if exists(c):
                    s = c.r % 2
                    act.wait_ge(x3_turned, c.n + 1)
                    if not known(c, 2):
                        act.wait_ge(stored[s], c.turn(2) * 32)
                    act.activation(x3n[:, s], p_n[s][:, :, :, :], ACT.Copy).then_inc(x3_read, 1)
                    act.wait_ge(x3_read, c.n + 1)
                    for half in range(2):
                        act.dma_start(pick(x3v, c.n)[:, half], x3n[:, s, half]).then_inc(stored[s], 16)

            schedule(act, step)
            for s in range(2):
                act.wait_ge(stored[s], 32 * (tiles // 2))

        @block.vector
        def _(dve):
            dve.wait_ge(bias_made, 1)
            dve.tensor_tensor(bias[:, :], b2s[:, :], p_bias[:, :], ALU.add).then_inc(bias_ready, 1)

            def step(t):
                a, b = t + 2, t + (-1)
                if exists(t):
                    s = t.r % 2
                    dve.wait_ge(v_made, t.n + 1)
                    if not known(t, 2):
                        dve.wait_ge(q_made, t.n - 1)
                        dve.wait_ge(r_mul, t.n - 1)
                    dve.wait_ge(z_made, t.n + 1)
                    dve.tensor_tensor(p[:, s, :, 1:COLS + 1], z[:, t.r % 4], v[:, s, :, 0:COLS], ALU.add).then_inc(p_made, 1)
                if exists(a):
                    slot = a.r
                    if known(a, 1):
                        dve.wait_ge(wrap_loaded, 16)
                    dve.wait_ge(loaded[slot], a.q * 32 + 32)
                    if not known(a, 4):
                        dve.wait_ge(p_made, a.n - 3)
                        dve.wait_ge(v_mul, a.n - 3)
                    src = 1 if isinstance(a.n, int) and a.n == tiles - 1 else 0
                    dve.scalar_tensor_tensor(out=z[:, a.r % 4], in0=xs[:, slot, src:src + 2], scalar=scale,
                                             in1=taus[:, slot], op0=ALU.mult, op1=ALU.add).then_inc(z_made, 1)
                if exists(b):
                    s = b.r % 2
                    dve.wait_ge(q_made, b.n + 1)
                    if not known(b, 2):
                        dve.wait_ge(x3_turned, b.n - 1)
                        dve.wait_ge(counted, b.n - 1)
                    dve.scalar_tensor_tensor(out=x3s[:, s], in0=xs[:, b.r, 1:3], scalar=shift,
                                             in1=q[:, s], op0=ALU.add, op1=ALU.add).then_inc(x3_made, 1)
                    dve.wait_ge(x3_made, b.n + 1)
                    dve.bn_stats(stats[:, (slice(b.n, b.n + 1) if isinstance(b.n, int) else bass.ds(b.n, 1)), :].squeeze(1),
                                 x3s[:, s].rearrange("p r w -> p (r w)")).then_inc(counted, 1)

            schedule(dve, step)


def wrap_halo(nc, x3):
    with ExitStack() as ctx:
        m = Scope(nc, ctx, "ha")
        sides, ends = m.sem("sides"), m.sem("ends")
        block = ctx.enter_context(nc.Block())
        inner = slice(HALO, HALO + ROWS)

        @block.sync
        def _(sp):
            sp.dma_start(x3[inner, 0:HALO], x3[inner, COLS:COLS + HALO]).then_inc(sides, 16)
            sp.dma_start(x3[inner, HALO + COLS:], x3[inner, HALO:2 * HALO]).then_inc(sides, 16)
            sp.wait_ge(sides, 32)
            sp.dma_start(x3[0:HALO], x3[ROWS:ROWS + HALO]).then_inc(ends, 16)
            sp.dma_start(x3[HALO + ROWS:PADDED_ROWS], x3[HALO:PADDED_ROWS - ROWS]).then_inc(ends, 16)
            sp.wait_ge(ends, 32)


SIDE = 2 * HALO + 1
KTAPS = SIDE * SIDE
SPOTS = PATCH * PATCH
WROWS = PATCH * WINDOW
PX = COLS // PATCH
BLOCK_PY = 4
BLOCKS = ROWS // PATCH // BLOCK_PY
SCAN = 8
SP_EPS = 1e-6
PLAIN = 1.0 - 0.5 ** SCAN


def patch_weights(nc, b_kernel, gate_kernel, selector, w_out, b_out, ident, patch_w, taps, ksum, w_plain, b_plain):
    with ExitStack() as ctx:
        m = Scope(nc, ctx, "kw")
        sel = m.sb("sel", [KTAPS, PATCH, 3 * PATCH - 1, WINDOW])
        kt = m.sb("kt", [KTAPS, 2, CH])
        tw = m.sb("tw", [WROWS, 2, CH, 2 * SPOTS])
        w = m.sb("w", [128, CH])
        epsm = m.sb("epsm", [128, 128])
        brow = m.sb("brow", [128, CH])
        p_t = m.ps("p_t", [KTAPS, 2, CH])
        p_w = [m.ps(f"p_w{i}", [WROWS, 2, 2, CH]) for i in range(4)]
        p_b = m.ps("p_b", [128, CH])
        loaded, k_turned, k_read, made, b_made = (m.sem(n) for n in ("loaded", "k_turned", "k_read", "made", "b_made"))
        even_read, odd_read, step, stored = (m.sem(n) for n in ("even_read", "odd_read", "step", "stored"))
        block = ctx.enter_context(nc.Block())
        pairs = 2 * SPOTS // 2

        @block.sync
        def _(sp):
            for f, kern in enumerate((b_kernel, gate_kernel)):
                sp.dma_start(taps[:, f, :], kern.rearrange("c a b -> c (a b)")).then_inc(loaded, 16)
            sp.dma_start(sel[:, :, :, :], selector).then_inc(loaded, 16)
            sp.dma_start(w[:, :], w_out).then_inc(loaded, 16)
            sp.dma_start(brow[:, :], b_out.rearrange("(a c) -> a c", a=1).to_broadcast((128, CH))).then_inc(loaded, 16)
            sp.wait_ge(even_read, pairs // 2)
            sp.wait_ge(odd_read, pairs // 2)
            for half in range(2):
                sp.dma_start(patch_w.rearrange("g p h c s -> h p g (c s)")[half],
                             tw[:, half].rearrange("p (g c) s -> p g (c s)", c=4)).then_inc(stored, 16)
            sp.wait_ge(stored, 32)

        @block.tensor
        def _(pe):
            pe.wait_ge(loaded, 16 * 5)
            for f in range(2):
                mm = pe.transpose(p_t[:, f, :], taps[:, f, :], ident[:, :])
            mm.then_inc(k_turned, 1)
            pe.wait_ge(k_read, 1)
            for n in range(pairs):
                half, spot = n // (SPOTS // 2), n % (SPOTS // 2) * 2
                if n >= 4:
                    pe.wait_ge((even_read, odd_read)[n % 2], (n - 4) // 2 + 1)
                for i in range(2):
                    oy, ox = divmod(spot + i, PATCH)
                    first = half * PATCH - oy + PATCH - 1
                    mm = pe.matmul(p_w[n % 4][:, i].rearrange("p f c -> p (f c)"),
                                   sel[:, ox, first:first + PATCH, :].rearrange("t a b -> t (a b)"),
                                   kt[:, :, :].rearrange("p f c -> p (f c)"), start=True, stop=True)
                mm.then_inc(made, 1)
            pe.wait_ge(step, 3)
            pe.matmul(p_b[:, :], epsm[:, :], w_plain, start=True, stop=True).then_inc(b_made, 1)

        def copies(eng, odd, copy, is_read):
            for n in range(odd, pairs, 2):
                half, spot = n // (SPOTS // 2), n % (SPOTS // 2) * 2
                eng.wait_ge(made, n + 1)
                for f in range(2):
                    done = copy(tw[:, half, :, f * SPOTS + spot:f * SPOTS + spot + 2].rearrange("p c s -> p s c"),
                                p_w[n % 4][:, :, f, :])
                done.then_inc(is_read, 1)

        @block.scalar
        def _(act):
            copies(act, 1, lambda out, in_: act.activation(out, in_, ACT.Copy), odd_read)

        @block.vector
        def _(dve):
            dve.wait_ge(k_turned, 1)
            dve.tensor_copy(kt[:, :, :], p_t[:, :, :]).then_inc(k_read, 1)
            dve.tensor_reduce(ksum, taps[:, :, :], mybir.AxisListType.X, ALU.add).then_inc(step, 1)
            dve.memset(epsm[:, :], SP_EPS).then_inc(step, 1)
            dve.tensor_scalar(w_plain, w[:, :], PLAIN, None, ALU.mult).then_inc(step, 1)
            copies(dve, 0, dve.tensor_copy, even_read)
            dve.wait_ge(b_made, 1)
            dve.tensor_tensor(b_plain, brow[:, :], p_b[:, :], ALU.add)


def depthwise_layer(nc, x3, patch_w, ksum, scale, shift, w_plain, b_plain, ident, out):
    groups = CH // 4
    LEAD = 4
    BEHIND = 3
    pairs = BLOCK_PY * PX // 8
    units = pairs // 2
    with ExitStack() as ctx:
        m = Scope(nc, ctx, "dw")
        xw = m.sb("xw", [WROWS, BLOCK_PY + 1, PX, CH])
        wts = m.sb("wts", [WROWS, 4, 2, 4, 2 * SPOTS])
        raw = m.sb("raw", [128, BLOCK_PY * PX, CH])
        nscale = m.sb("nscale", [128, 1])
        f_shift = m.sb("f_shift", [128, 2])
        gate = m.sb("gate", [128, 2, 2, 4 * SPOTS])
        val = m.sb("val", [128, 2, 2, 4 * SPOTS])
        bt = m.sb("bt", [128, 4, BANK])
        soft = m.sb("soft", [128, 2, BANK])
        hid = m.sb("hid", [128, 2, PATCH, 128])
        xr = m.sb("xr", [128, 2, PATCH, CH])
        outs = m.sb("outs", [128, 2, PATCH, CH])
        p_conv = [m.ps(f"p_conv{i}", [128, 4, BLOCK_PY * PX]) for i in range(2)]
        p_turn = m.ps("p_turn", [128, 2, 2, 2, PATCH, 4, PATCH])
        p_out = [m.ps(f"p_out{i}", [128, 4, CH]) for i in range(2)]
        x_loaded = m.sem("x_loaded")
        w_loaded = [m.sem(f"w_loaded{i}") for i in range(4)]
        r_loaded = [m.sem(f"r_loaded{i}") for i in range(2)]
        stored = [m.sem(f"stored{i}") for i in range(2)]
        biased = m.sem("biased")
        prepared, conved, even_read, odd_read = (m.sem(n) for n in ("prepared", "conved", "even_read", "odd_read"))
        turned, gate_step, val_made = (m.sem(n) for n in ("turned", "gate_step", "val_made"))
        bt_made, abs_made, soft_step = (m.sem(n) for n in ("bt_made", "abs_made", "soft_step"))
        pe_passed = m.sem("pe_passed")
        hid_made, out_made, added = (m.sem(n) for n in ("hid_made", "out_made", "added"))
        block = ctx.enter_context(nc.Block())
        x_at = x3.tensor
        line = PADDED * CH

        def window(patch_row, y):
            return bass.AP(x_at, patch_row * (PATCH * line) + y * line, [[CH, WINDOW], [PATCH * CH, PX], [1, CH]])

        def unit_rows(tensor, row_len, pad, b, n):
            y, x = n // 2 * PATCH + pad, n % 2 * 128 + pad
            return bass.AP(tensor, b * (BLOCK_PY * PATCH * row_len * CH) + (y * row_len + x) * CH,
                           [[CH, 128], [row_len * CH, PATCH], [1, CH]])

        def turns(b, u):
            return b * pairs + u

        @block.sync
        def _(sp):
            def load_windows(b, r):
                for y in range(PATCH):
                    sp.dma_start(xw[y * WINDOW:(y + 1) * WINDOW, r], window(b * BLOCK_PY + r, y)).then_inc(x_loaded, 16)

            def load_residual(b, n):
                sp.dma_start(xr[:, n % 2], unit_rows(x_at, PADDED, HALO, b, n)).then_inc(r_loaded[n % 2], 16)

            def one_block(b, last):
                with sp.Fori(0, groups // 4) as i:
                    for k in range(4):
                        sp.wait_ge(conved, b * groups + i * 4 + (k + 1))
                        sp.dma_start(wts[:, k], pick(patch_w, i * 4 + k)).then_inc(w_loaded[k], 16)
                sp.wait_ge(added, b * pairs)
                load_residual(b, 0)
                load_residual(b, 1)
                sp.wait_ge(conved, b * groups + (groups + LEAD))
                for n in range(units):
                    if not last and n <= BLOCK_PY:
                        load_windows(b + 1, n)
                    sp.wait_ge(added, turns(b, 2 * n + 2))
                    sp.dma_start(unit_rows(out.tensor, COLS, 0, b, n), outs[:, n % 2]).then_inc(stored[n % 2], 16)
                    if n < units - 2:
                        load_residual(b, n + 2)

            for r in range(BLOCK_PY + 1):
                load_windows(0, r)
            with sp.Fori(0, BLOCKS - 1) as b:
                one_block(b, False)
            one_block(BLOCKS - 1, True)
            for p in range(2):
                sp.wait_ge(stored[p], 16 * BLOCKS * units // 2)

        @block.tensor
        def _(pe):
            with pe.Fori(0, BLOCKS) as b:
                pe.wait_ge(x_loaded, (b + 1) * (16 * PATCH * (BLOCK_PY + 1)))
                pe.sem_inc(pe_passed, 1)
                with pe.Fori(0, groups // 4) as i:
                    for k in range(4):
                        pe.wait_ge(w_loaded[k], b * (4 * groups) + i * 16 + 16)
                        pe.wait_ge((even_read, odd_read)[k % 2], b * (groups // 2) + i * 2 + k // 2)
                        for j in range(4):
                            for half in range(2):
                                mm = pe.matmul(p_conv[k % 2][:, j, :], wts[:, k, half, j, :],
                                               xw[:, half:half + BLOCK_PY, :, bass.ds(i * 16 + (k * 4 + j), 1)].squeeze(3),
                                               start=half == 0, stop=half == 1)
                        mm.then_inc(conved, 1)
                pe.wait_ge(even_read, b * (groups // 2) + groups // 2)
                pe.wait_ge(odd_read, b * (groups // 2) + groups // 2)
                for u in range(pairs + 5):
                    if u < pairs:
                        pe.wait_ge(val_made, turns(b, u - 1) if u else turns(b, 0))
                        for g in range(2):
                            for x in range(4):
                                mm = pe.transpose(p_turn[:, u % 2, g, :, :, x, :], raw[:, u * 8 + g * 4 + x, :], ident[:, :])
                        mm.then_inc(turned, 1)
                    v = u - 5
                    if v >= 0:
                        pe.wait_ge(hid_made, turns(b, v // 2 * 2 + 2))
                        pe.wait_ge(added, turns(b, v - 1) if v else turns(b, 0))
                        for y in range(4):
                            mm = pe.matmul(p_out[v % 2][:, y, :], hid[:, v // 2 % 2, v % 2 * 4 + y, :], w_plain,
                                           start=True, stop=True)
                        mm.then_inc(out_made, 1)

        def copy_raw(eng, b, i, k, copy, is_read):
            eng.wait_ge(conved, b * groups + i * 4 + (k + 1 + LEAD))
            copy(raw[:, :, bass.ds(i * 16 + k * 4, 4)].rearrange("s p c -> s c p"), p_conv[k % 2][:, :, :]).then_inc(is_read, 1)

        @block.scalar
        def _(act):
            act.preload_act_table_set(EXP_LN_SET)
            act.wait_ge(prepared, 3)
            with act.Fori(0, BLOCKS) as b:
                with act.Fori(0, groups // 4) as i:
                    for k in (1, 3):
                        copy_raw(act, b, i, k, lambda out, in_: act.activation(out, in_, ACT.Copy), odd_read)
                for u in range(pairs + 2):
                    v = u - 2
                    g = gate[:, u % 2]
                    if u < pairs:
                        act.wait_ge(turned, turns(b, u + 1))
                        act.wait_ge(bt_made, turns(b, u - 1) if u else turns(b, 0))
                        act.activation(g, p_turn[:, u % 2].rearrange("c g f a x d -> c f g (a x d)")[:, 1], ACT.Exp,
                                       bias=f_shift[:, 1:2], scale=nscale[:, :]).then_inc(gate_step, 1)
                    if v >= 0:
                        act.wait_ge(abs_made, turns(b, v + 1))
                        act.activation(soft[:, v % 2, :], soft[:, v % 2, :], ACT.Exp, scale=-1.0).then_inc(soft_step, 1)
                    if u < pairs:
                        act.wait_ge(gate_step, turns(b, u) * 3 + 1)
                        act.activation(g, g, ACT.Ln, bias=1.0).then_inc(gate_step, 1)
                    if v >= 0:
                        act.wait_ge(soft_step, turns(b, v) * 2 + 1)
                        act.activation(soft[:, v % 2, :], soft[:, v % 2, :], ACT.Ln, bias=1.0).then_inc(soft_step, 1)
                    if u < pairs:
                        act.wait_ge(gate_step, turns(b, u) * 3 + 2)
                        act.activation(g, g, ACT.Exp, scale=-1.0).then_inc(gate_step, 1)

        @block.gpsimd
        def _(pool):
            with pool.Fori(0, BLOCKS) as b:
                for u in range(pairs + BEHIND):
                    if u < pairs:
                        pool.wait_ge(gate_step, turns(b, u) * 3 + 3)
                        pool.wait_ge(val_made, turns(b, u + 1))
                        pool.wait_ge(hid_made, turns(b, u - 3) if u > 3 else turns(b, 0))
                        by_bank = "c g (y t) -> c g y t"
                        pool.tensor_tensor(bt[:, u % 4, :].rearrange("c (y g t) -> c g y t", g=2, t=32),
                                           gate[:, u % 2].rearrange(by_bank, t=32), val[:, u % 2].rearrange(by_bank, t=32),
                                           ALU.mult).then_inc(bt_made, 1)
                    w = u - BEHIND
                    if w >= 0:
                        n, half = w // 2, slice(w % 2 * 4, w % 2 * 4 + 4)
                        pool.wait_ge(r_loaded[n % 2], b * (8 * units) + n // 2 * 16 + 16)
                        pool.tensor_tensor(xr[:, n % 2, half], xr[:, n % 2, half],
                                           b_plain.unsqueeze(1).broadcast_to((128, 4, CH)), ALU.add).then_inc(biased, 1)

        @block.vector
        def _(dve):
            dve.tensor_scalar(nscale[:, :], scale, -1.0, None, ALU.mult).then_inc(prepared, 1)
            dve.tensor_scalar(f_shift[:, 0:1], ksum[:, 0:1], shift, None, ALU.mult).then_inc(prepared, 1)
            dve.tensor_scalar(f_shift[:, 1:2], ksum[:, 1:2], shift, -1.0, ALU.mult, ALU.mult).then_inc(prepared, 1)
            dve.wait_ge(prepared, 3)
            dve.memset(bt[:, 0, 0:1], 0.0).then_inc(conved, LEAD)

            with dve.Fori(0, BLOCKS) as b:
                with dve.Fori(0, groups // 4) as i:
                    for k in (0, 2):
                        copy_raw(dve, b, i, k, dve.tensor_copy, even_read)
                for u in range(pairs + 4):
                    if u < pairs:
                        dve.wait_ge(gate_step, turns(b, u) * 3 + 1)
                        dve.wait_ge(bt_made, turns(b, u - 1) if u else turns(b, 0))
                        dve.tensor_scalar(val[:, u % 2], p_turn[:, u % 2].rearrange("c g f a x d -> c f g (a x d)")[:, 0],
                                          scale, f_shift[:, 0:1], ALU.mult, ALU.add).then_inc(val_made, 1)
                    v = u - 1
                    if 0 <= v < pairs:
                        dve.wait_ge(bt_made, turns(b, v + 1))
                        dve.wait_ge(hid_made, turns(b, v - 1) if v else turns(b, 0))
                        dve.scalar_tensor_tensor(out=soft[:, v % 2, :], in0=bt[:, v % 4, :], scalar=-1.0, in1=bt[:, v % 4, :],
                                                 op0=ALU.mult, op1=ALU.max).then_inc(abs_made, 1)
                    v = u - 2
                    if 0 <= v < pairs:
                        p = v % 2
                        dve.wait_ge(soft_step, turns(b, v) * 2 + 2)
                        if v >= 4:
                            dve.wait_ge(out_made, turns(b, v // 2 * 2 - 2))
                        dve.scalar_tensor_tensor(out=hid[:, v // 2 % 2, :, p * 64:p * 64 + 64],
                                                 in0=bt[:, v % 4, :].rearrange("c (y t) -> c y t", t=64), scalar=0.0,
                                                 in1=soft[:, p, :].rearrange("c (y t) -> c y t", t=64),
                                                 op0=ALU.max, op1=ALU.add).then_inc(hid_made, 1)
                    w = u - 4
                    if w >= 0:
                        n = w // 2
                        dve.wait_ge(out_made, turns(b, w + 1))
                        dve.wait_ge(biased, turns(b, w + 1))
                        dve.wait_ge(stored[n % 2], b * (8 * units) + n // 2 * 16)
                        half = slice(w % 2 * 4, w % 2 * 4 + 4)
                        dve.tensor_tensor(outs[:, n % 2, half], p_out[w % 2][:, :, :], xr[:, n % 2, half],
                                          ALU.add).then_inc(added, 1)


def origin_patch(nc, x3, a_kernel, gate_a_kernel, taps, ksum, scale, shift, w_out, b_out, ident, out):
    span = SIDE + 2 * HALO
    n_tok = KTAPS
    pieces = []
    for row in range(span):
        y = row + ROWS - HALO if row < 2 * HALO else row - HALO
        for x, first, left in ((COLS - HALO, 0, 2 * HALO), (HALO, 2 * HALO, SIDE)):
            at = row * span + first
            while left:
                k = min(left, 128 - at % 128)
                pieces.append((at, y, x, k))
                at, x, left = at + k, x + k, left - k
    with ExitStack() as ctx:
        m = Scope(nc, ctx, "og")
        xs = m.sb("xs", [128, 2, CH])
        win = m.sb("win", [128, 2, 128])
        kern = m.sb("kern", [128, 2, n_tok])
        ga_sum = m.sb("ga_sum", [128, 1])
        conv = m.sb("conv", [128, 3, n_tok])
        add = m.sb("add", [128, 3])
        gated = m.sb("gated", [128, 3, n_tok])
        b_sig, a_sig, tmp = (m.sb(n, [128, n_tok]) for n in ("b_sig", "a_sig", "tmp"))
        bt, gate, soft, hid = (m.sb(n, [128, n_tok]) for n in ("bt", "gate", "soft", "hid"))
        z, c, c2, c4, series = (m.sb(n, [128, n_tok]) for n in ("z", "c", "c2", "c4", "series"))
        w = m.sb("w", [128, CH])
        bias = m.sb("bias", [n_tok, CH])
        res = m.sb("res", [n_tok, CH])
        final = m.sb("final", [n_tok, CH])
        p_t = m.ps("p_t", [128, 2, 128])
        p_o = m.ps("p_o", [n_tok, CH])
        loaded, cleared, turned, stored = (m.sem(n) for n in ("loaded", "cleared", "turned", "stored"))
        dve_step, act_step = m.sem("dve_step"), m.sem("act_step")
        conv_ready, sig_ready, gate_ready, series_ready = (m.sem(n) for n in ("conv_ready", "sig_ready", "gate_ready", "series_ready"))
        hid_ready, out_made, final_ready = (m.sem(n) for n in ("hid_ready", "out_made", "final_ready"))
        block = ctx.enter_context(nc.Block())
        loads = len(pieces) + 4 + 2 * SIDE

        @block.sync
        def _(sp):
            sp.wait_ge(cleared, 1)
            for at, y, x, k in pieces:
                sp.dma_start(xs[at % 128:at % 128 + k, at // 128, :], x3[y, x:x + k]).then_inc(loaded, 16)
            for i, kn in enumerate((a_kernel, gate_a_kernel)):
                sp.dma_start(kern[:, i, :], kn.rearrange("c a b -> c (a b)")).then_inc(loaded, 16)
            sp.dma_start(w[:, :], w_out).then_inc(loaded, 16)
            sp.dma_start(bias[:, :], b_out.rearrange("(a c) -> a c", a=1).to_broadcast((n_tok, CH))).then_inc(loaded, 16)
            for i in range(SIDE):
                y = (i - HALO) % ROWS + HALO
                sp.dma_start(res[i * SIDE:i * SIDE + HALO, :], x3[y, COLS:COLS + HALO]).then_inc(loaded, 16)
                sp.dma_start(res[i * SIDE + HALO:(i + 1) * SIDE, :], x3[y, HALO:2 * HALO + 1]).then_inc(loaded, 16)
            sp.wait_ge(final_ready, 1)
            for i in range(SIDE):
                y = (i - HALO) % ROWS
                sp.dma_start(out[0, y, COLS - HALO:COLS], final[i * SIDE:i * SIDE + HALO, :]).then_inc(stored, 16)
                sp.dma_start(out[0, y, 0:HALO + 1], final[i * SIDE + HALO:(i + 1) * SIDE, :]).then_inc(stored, 16)
            sp.wait_ge(stored, 32 * SIDE)

        @block.gpsimd
        def _(pool):
            pool.memset(xs[:, :, :], 0.0).then_inc(cleared, 1)

        @block.tensor
        def _(pe):
            pe.wait_ge(loaded, 16 * loads)
            for i in range(2):
                mm = pe.transpose(p_t[:, i, :], xs[:, i, :], ident[:, :])
            mm.then_inc(turned, 1)
            pe.wait_ge(hid_ready, 1)
            pe.matmul(p_o[:, :], hid[:, :], w[:, :], start=True, stop=True).then_inc(out_made, 1)

        @block.scalar
        def _(act):
            act.preload_act_table_set(EXP_LN_SET)
            done = 0

            def apply(out, in_, f, signal=None, **kw):
                nonlocal done
                act.wait_ge(act_step, done)
                a = act.activation(out, in_, f, **kw)
                if signal is None:
                    a.then_inc(act_step, 1)
                    done += 1
                else:
                    a.then_inc(signal, 1)

            def sigmoid(out, in_, sign, signal=None):
                apply(tmp[:, :], in_, ACT.Exp, scale=-sign)
                apply(tmp[:, :], tmp[:, :], ACT.Ln, bias=1.0)
                apply(out, tmp[:, :], ACT.Exp, scale=-1.0, signal=signal)

            act.wait_ge(conv_ready, 1)
            sigmoid(b_sig[:, :], gated[:, 1, :], 1.0)
            sigmoid(a_sig[:, :], gated[:, 2, :], 1.0, sig_ready)
            act.wait_ge(gate_ready, 1)
            act.wait_ge(sig_ready, 1)
            sigmoid(z[:, :], gate[:, :], 1.0)
            sigmoid(c[:, :], gate[:, :], -1.0)
            apply(c2[:, :], c[:, :], ACT.Square)
            apply(c4[:, :], c2[:, :], ACT.Square)
            apply(soft[:, :], soft[:, :], ACT.Exp, scale=-1.0)
            apply(soft[:, :], soft[:, :], ACT.Ln, bias=1.0, signal=series_ready)

        @block.vector
        def _(dve):
            done = 0

            def chained(instruction):
                nonlocal done
                instruction.then_inc(dve_step, 1)
                done += 1

            def grid(ap):
                return ap.rearrange("c (a b) -> c a b", b=SIDE)

            dve.wait_ge(turned, 1)
            chained(dve.tensor_copy(win[:, :, :], p_t[:, :, :]))
            chained(dve.memset(conv[:, :, :], 0.0))
            chained(dve.tensor_reduce(ga_sum[:, :], kern[:, 1, :], mybir.AxisListType.X, ALU.add))
            field = win[:, :, :].rearrange("c a b -> c (a b)")[:, 0:span * span].rearrange("c (a b) -> c a b", b=span)
            for tap in range(KTAPS):
                ty, tx = divmod(tap, SIDE)
                dve.wait_ge(dve_step, done)
                for f, k in enumerate((taps[:, 0, tap:tap + 1], taps[:, 1, tap:tap + 1], kern[:, 1, tap:tap + 1])):
                    chained(dve.scalar_tensor_tensor(
                        out=grid(conv[:, f, :]), in0=field[:, SIDE - 1 - ty:2 * SIDE - 1 - ty, SIDE - 1 - tx:2 * SIDE - 1 - tx],
                        scalar=k, in1=grid(conv[:, f, :]), op0=ALU.mult, op1=ALU.add))
            dve.wait_ge(dve_step, done)
            chained(dve.tensor_scalar(add[:, 0:2], ksum, shift, None, ALU.mult))
            chained(dve.tensor_scalar(add[:, 2:3], ga_sum[:, :], shift, None, ALU.mult))
            dve.wait_ge(dve_step, done)
            for f in range(3):
                last = dve.tensor_scalar(gated[:, f, :], conv[:, f, :], scale, add[:, f:f + 1], ALU.mult, ALU.add)
                last.then_inc(conv_ready if f == 2 else dve_step, 1)
            done += 2
            dve.wait_ge(sig_ready, 1)
            chained(dve.tensor_tensor(bt[:, :], gated[:, 0, :], b_sig[:, :], ALU.mult))
            chained(dve.tensor_tensor(gate[:, :], kern[:, 0, :], a_sig[:, :], ALU.mult))
            dve.wait_ge(dve_step, done)
            dve.scalar_tensor_tensor(out=soft[:, :], in0=bt[:, :], scalar=-1.0, in1=bt[:, :],
                                     op0=ALU.mult, op1=ALU.max).then_inc(gate_ready, 1)
            dve.wait_ge(series_ready, 1)
            chained(dve.scalar_tensor_tensor(out=soft[:, :], in0=bt[:, :], scalar=0.0, in1=soft[:, :],
                                             op0=ALU.max, op1=ALU.add))
            for x, y in ((c, z), (c2, series), (c4, series)):
                chained(dve.scalar_tensor_tensor(out=series[:, :], in0=x[:, :], scalar=1.0, in1=y[:, :],
                                                 op0=ALU.add, op1=ALU.mult))
                dve.wait_ge(dve_step, done)
            dve.scalar_tensor_tensor(out=hid[:, :], in0=soft[:, :], scalar=SP_EPS, in1=series[:, :],
                                     op0=ALU.add, op1=ALU.mult).then_inc(hid_ready, 1)
            dve.wait_ge(out_made, 1)
            chained(dve.tensor_tensor(final[:, :], p_o[:, :], bias[:, :], ALU.add))
            dve.wait_ge(dve_step, done)
            dve.tensor_tensor(final[:, :], final[:, :], res[:, :], ALU.add).then_inc(final_ready, 1)


def build(nc, x, kv_x, tri_bias, mask_bias, wq, wk, wv, wg, wo, w1, w2, ff_w0, ff_b0, ff_w1, ff_b1, ln_g, ln_b,
          c_w1, c_b1, c_w2, c_b2, a_kernel, b_kernel, gate_a, gate_b, w_out, b_out,
          identity, group_mean, forward, inverse_rows, inverse_cols, selector, out):
    def scratch(name, shape):
        return nc.dram_tensor(name, shape, FP32).ap()

    x1 = scratch("x1", [ROWS, COLS, CH])
    x2 = scratch("x2", [CH, TOKENS])
    x3 = scratch("x3", [PADDED_ROWS, PADDED, CH])
    spec = [scratch(f"spec{a}", [PARTS, ROWS, CH]) for a in range(2)]
    mixed = [scratch(f"mixed{a}", [ROWS, PARTS, CH]) for a in range(2)]
    taps_d = scratch("taps_d", [TAPS, TOKENS])
    convs = [scratch(f"convs{a}", [ROWS, COLS]) for a in range(2)]
    tau = scratch("tau", [TOKENS])
    patch_w = scratch("patch_w", [CH // 4, WROWS, 2, 4, 2 * SPOTS])
    with ExitStack() as ctx:
        m = Scope(nc, ctx, "all")
        ident = m.sb("ident", [128, 128])
        gmean = m.sb("gmean", [128, 128])
        coef = m.sb("coef", [128, 2])
        scale, shift = coef[:, 0:1], coef[:, 1:2]
        const_loaded = m.sem("const_loaded")
        with nc.Block() as block:
            @block.sync
            def _(sp):
                sp.dma_start(ident[:, :], identity).then_inc(const_loaded, 16)
                sp.dma_start(gmean[:, :], group_mean).then_inc(const_loaded, 16)
                sp.wait_ge(const_loaded, 32)

        def coefficients(name, stats):
            group_norm_coefficients(nc, name, stats[:, :, :].rearrange("p a b -> p (a b)"), gmean[:, :], scale, shift)

        with nc.sbuf_tensor("stats0", [128, TOKENS // BANK, 6], FP32) as stats:
            input_statistics(nc, x, ident, stats)
            coefficients("l0", stats)
        attention(nc, x, kv_x, tri_bias, mask_bias, wq, wk, wv, wg, wo, ident, scale, shift, x1)
        with nc.sbuf_tensor("stats2", [128, TOKENS // BANK, 6], FP32) as stats:
            consts = {"forward": forward, "inverse_rows": inverse_rows, "inverse_cols": inverse_cols}
            fourier_layer(nc, x1, w1, w2, ff_w0, ff_b0, ff_w1, ff_b1, ln_g, ln_b, consts, ident, gmean[:, :], coef,
                          spec, mixed, x2, stats)
            coefficients("l2", stats)
        row_taps(nc, x2, c_w1, scale, shift, taps_d)
        one_channel_part(nc, taps_d, c_w1, c_b1, convs, tau)
        with nc.sbuf_tensor("stats3", [128, TOKENS // BANK, 6], FP32) as stats:
            pointwise_part(nc, x2, tau, c_w2, c_b2, scale, shift, ident, x3, stats)
            wrap_halo(nc, x3)
            coefficients("l3", stats)
        taps = m.sb("taps", [128, 2, KTAPS])
        ksum = m.sb("ksum", [128, 2])
        w_plain = m.sb("w_plain", [128, CH])
        b_plain = m.sb("b_plain", [128, CH])
        patch_weights(nc, b_kernel, gate_b, selector, w_out, b_out, ident, patch_w, taps, ksum[:, :],
                      w_plain[:, :], b_plain[:, :])
        depthwise_layer(nc, x3, patch_w, ksum, scale, shift, w_plain[:, :], b_plain[:, :], ident, out)
        origin_patch(nc, x3, a_kernel, gate_a, taps, ksum[:, :], scale, shift, w_out, b_out, ident, out)


def constants():
    angle = 2 * np.pi / COLS * np.arange(COLS)[:, None] * np.arange(MODES)[None, :]
    root = COLS ** 0.5
    forward = np.zeros((COLS, PARTS))
    forward[:, 0::2] = np.cos(angle) / root
    forward[:, 1::2] = -np.sin(angle) / root
    inverse = np.zeros((PARTS, COLS))
    weight = np.where(np.arange(MODES) == 0, 1, 2)[:, None] / root
    inverse[0::2] = weight * np.cos(angle.T)
    inverse[1::2] = -weight * np.sin(angle.T)
    inverse[1] = 0
    rows = np.zeros((2, 4, PARTS, 4, 128))
    for half in range(2):
        for n in range(4):
            rows[half, n, :, n] = inverse[:, half * 128:(half + 1) * 128]
    cols = np.zeros((4, PARTS, 2, 2, COLS))
    for n in range(4):
        cols[n, :, n // 2, n % 2] = inverse
    selector = np.zeros((KTAPS, PATCH, 3 * PATCH - 1, WINDOW))
    for tap in range(KTAPS):
        ty, tx = divmod(tap, SIDE)
        for ox in range(PATCH):
            selector[tap, ox, PATCH - 1 + 2 * HALO - ty, 2 * HALO - tx + ox] = 1
    found = dict(identity=np.eye(128), group_mean=np.kron(np.eye(32), np.full((4, 4), 0.25)), forward=forward,
                 inverse_rows=rows.reshape(2, 128, 4, 128), inverse_cols=cols.reshape(128, 2, BANK), selector=selector)
    return {n: np.ascontiguousarray(v, dtype=np.float32) for n, v in found.items()}


_INS = ["x", "L0_conv_kv_x", "L0_conv_tri_bias", "L0_conv_mask_bias", "L0_conv_Wq", "L0_conv_Wk", "L0_conv_Wv",
        "L0_conv_Wg", "L0_conv_Wo", "L1_conv_w1", "L1_conv_w2", "L1_conv_ff_w0", "L1_conv_ff_b0", "L1_conv_ff_w1",
        "L1_conv_ff_b1", "L1_conv_ln_g", "L1_conv_ln_b", "L2_conv_w1", "L2_conv_b1", "L2_conv_w2", "L2_conv_b2",
        "L3_conv_A_kernel", "L3_conv_B_kernel", "L3_conv_gate_A_kernel", "L3_conv_gate_B_kernel", "L3_conv_W_out",
        "L3_conv_b_out"]


def kernel(**inputs):
    import concourse.bacc as _bacc
    from concourse import mybir as _mybir
    from concourse.bass_utils import run_bass_kernel_spmd as _run

    nc = _bacc.Bacc("TRN2", target_bir_lowering=False, num_devices=1)
    arrays, args = {}, []
    given = {name: np.ascontiguousarray(inputs[name]) for name in _INS}
    given.update(constants())
    for name, a in given.items():
        arrays[f"in_{name}_dram"] = a
        args.append(nc.dram_tensor(f"in_{name}_dram", a.shape, _mybir.dt.from_np(a.dtype), kind="ExternalInput").ap())
    args.append(nc.dram_tensor("out_0_dram", (1, ROWS, COLS, CH), FP32, kind="ExternalOutput").ap())
    build(nc, *args)
    r = _run(nc, [arrays], core_ids=[0])
    return r.results[0]["out_0_dram"]
```
